# Optimizing a Trainium2 kernel written in Bass

```python
import numpy as np
import jax
import jax.numpy as jnp

def _softmax(x, axis=-1):
    return jax.nn.softmax(x, axis=axis)

def _gelu(x):
    return jax.nn.gelu(x, approximate=True)

def _silu(x):
    return jax.nn.silu(x)

def _sigmoid(x):
    return jax.nn.sigmoid(x)

def _layernorm(x, axis=-1, eps=1e-05):
    m = jnp.mean(x, axis=axis, keepdims=True)
    v = jnp.var(x, axis=axis, keepdims=True)
    return (x - m) / jnp.sqrt(v + eps)

def _scatter_add(tgt, idx, src, axis=0):
    return tgt.at[idx].add(src)

def _segment_sum(src, seg, n):
    return jax.ops.segment_sum(src, seg, n)
kernel_name = 'mk_prb_d1_jaxref_r4_bec89c'

def setup_inputs(seed: int=0):
    np.random.seed(seed)
    _w = jnp.asarray

    def _L0_attn_setup():
        import math
        import jax, jax.numpy as jnp
        import numpy as np
        HID = 256
        H = 8
        D = HID // H
        CHUNK = 12
        PAST = 13 - 1
        FUT = 0
        CTX = CHUNK + PAST + FUT
        SOFTCAP = 50.0
        Q_SCALE = D ** (-0.5) / math.log(2)
        K_SCALE = math.log(1.0 + math.e) / math.log(2)

        def _extract_block_context(x, num_blocks):
            xp = jnp.pad(x, ((0, 0), (PAST, FUT + CHUNK - 1), (0, 0), (0, 0)))
            idx = jnp.arange(num_blocks)[:, None] * CHUNK + jnp.arange(CTX)[None, :]
            return xp[:, idx]

        def _rel_shift(x):
            B, Hh, nb, bs, pos_len = x.shape
            x = jnp.pad(x, ((0, 0), (0, 0), (0, 0), (0, 0), (0, CTX + 1 - pos_len)))
            x = x.reshape(B, Hh, nb, bs * (CTX + 1))[..., :bs * CTX]
            return x.reshape(B, Hh, nb, bs, CTX)
        key = jax.random.key(seed)
        ks = jax.random.split(key, 8)
        B, S = (4, 1536)
        P = CTX + 1
        std = HID ** (-0.5)
        return {'hidden_states': jax.random.normal(ks[0], (B, S, HID), jnp.float32), 'position_embeddings': jax.random.normal(ks[1], (P, HID), jnp.float32), 'Wq': jax.random.normal(ks[2], (HID, HID), jnp.float32) * std, 'Wk': jax.random.normal(ks[3], (HID, HID), jnp.float32) * std, 'Wv': jax.random.normal(ks[4], (HID, HID), jnp.float32) * std, 'Wpost': jax.random.normal(ks[5], (HID, HID), jnp.float32) * std, 'Wrel': jax.random.normal(ks[6], (HID, HID), jnp.float32) * std, 'per_dim_scale': jnp.zeros((D,), jnp.float32)}
    _L0_attn_in = _L0_attn_setup()

    def _L0_ffn_setup():
        import jax, jax.numpy as jnp
        import numpy as np
        DIM = 256
        HID = 704
        E = 8
        TOP_K = 2
        EPS = 1e-06

        def _rmsnorm(x, w):
            var = jnp.mean(jnp.square(x), axis=-1, keepdims=True)
            return x * jax.lax.rsqrt(var + EPS) * w
        key = jax.random.key(seed)
        ks = jax.random.split(key, 5)
        x = jax.random.normal(ks[0], (4, 512, DIM), dtype=jnp.float32)
        norm_weight = jnp.ones((DIM,), dtype=jnp.float32)
        router_weight = jax.random.normal(ks[1], (E, DIM), dtype=jnp.float32) * 0.02
        gate_up_weight = jax.random.normal(ks[2], (E, 2 * HID, DIM), dtype=jnp.float32) * (0.02 / np.sqrt(E))
        down_weight = jax.random.normal(ks[3], (E, DIM, HID), dtype=jnp.float32) * (0.02 / np.sqrt(E))
        residual_alpha = jnp.float32(1.0)
        return {'x': x, 'norm_weight': norm_weight, 'router_weight': router_weight, 'gate_up_weight': gate_up_weight, 'down_weight': down_weight, 'residual_alpha': residual_alpha}
    _L0_ffn_in = _L0_ffn_setup()
    _d = {'L0_attn_hidden_states': _L0_attn_in['hidden_states'], 'L0_attn_position_embeddings': _L0_attn_in['position_embeddings'], 'L0_attn_Wq': _L0_attn_in['Wq'], 'L0_attn_Wk': _L0_attn_in['Wk'], 'L0_attn_Wv': _L0_attn_in['Wv'], 'L0_attn_Wpost': _L0_attn_in['Wpost'], 'L0_attn_Wrel': _L0_attn_in['Wrel'], 'L0_attn_per_dim_scale': _L0_attn_in['per_dim_scale'], 'L0_ffn_norm_weight': _L0_ffn_in['norm_weight'], 'L0_ffn_router_weight': _L0_ffn_in['router_weight'], 'L0_ffn_gate_up_weight': _L0_ffn_in['gate_up_weight'], 'L0_ffn_down_weight': _L0_ffn_in['down_weight'], 'L0_ffn_residual_alpha': _L0_ffn_in['residual_alpha']}
    _x0 = _d['L0_attn_hidden_states']
    _d['L0_attn_hidden_states'] = jax.random.normal(jax.random.fold_in(jax.random.key(seed), 1), (1, 4096, 256), dtype=_x0.dtype)
    del _x0
    return _d

def reference(L0_attn_hidden_states, L0_attn_position_embeddings, L0_attn_Wq, L0_attn_Wk, L0_attn_Wv, L0_attn_Wpost, L0_attn_Wrel, L0_attn_per_dim_scale, L0_ffn_norm_weight, L0_ffn_router_weight, L0_ffn_gate_up_weight, L0_ffn_down_weight, L0_ffn_residual_alpha):

    def _L0_attn_ref(hidden_states, position_embeddings, Wq, Wk, Wv, Wpost, Wrel, per_dim_scale):
        import math
        import jax, jax.numpy as jnp
        import numpy as np
        HID = 256
        H = 8
        D = HID // H
        CHUNK = 12
        PAST = 13 - 1
        FUT = 0
        CTX = CHUNK + PAST + FUT
        SOFTCAP = 50.0
        Q_SCALE = D ** (-0.5) / math.log(2)
        K_SCALE = math.log(1.0 + math.e) / math.log(2)

        def _extract_block_context(x, num_blocks):
            xp = jnp.pad(x, ((0, 0), (PAST, FUT + CHUNK - 1), (0, 0), (0, 0)))
            idx = jnp.arange(num_blocks)[:, None] * CHUNK + jnp.arange(CTX)[None, :]
            return xp[:, idx]

        def _rel_shift(x):
            B, Hh, nb, bs, pos_len = x.shape
            x = jnp.pad(x, ((0, 0), (0, 0), (0, 0), (0, 0), (0, CTX + 1 - pos_len)))
            x = x.reshape(B, Hh, nb, bs * (CTX + 1))[..., :bs * CTX]
            return x.reshape(B, Hh, nb, bs, CTX)
        B, S, _ = hidden_states.shape
        nb = (S + CHUNK - 1) // CHUNK
        pad = nb * CHUNK - S
        q = (hidden_states @ Wq.T).reshape(B, S, H, D)
        k = (hidden_states @ Wk.T).reshape(B, S, H, D)
        v = (hidden_states @ Wv.T).reshape(B, S, H, D)
        q = q * (Q_SCALE * jax.nn.softplus(per_dim_scale))
        k = k * K_SCALE
        q_blocked = jnp.pad(q, ((0, 0), (0, pad), (0, 0), (0, 0))).reshape(B, nb, CHUNK, H, D)
        k_ctx = _extract_block_context(k, nb)
        v_ctx = _extract_block_context(v, nb)
        matrix_ac = jnp.einsum('bnchd,bnkhd->bhnck', q_blocked, k_ctx)
        rel_k = (position_embeddings @ Wrel.T).reshape(-1, H, D)
        matrix_bd = jnp.einsum('bnchd,phd->bhncp', q_blocked, rel_k)
        matrix_bd = _rel_shift(matrix_bd)
        logits = matrix_ac + matrix_bd
        logits = jnp.tanh(logits / SOFTCAP) * SOFTCAP
        attn = jax.nn.softmax(logits, axis=-1)
        out = jnp.einsum('bhnck,bnkhd->bnchd', attn, v_ctx)
        out = out.reshape(B, nb * CHUNK, H * D)[:, :S]
        return out @ Wpost.T

    def _L0_ffn_ref(x, norm_weight, router_weight, gate_up_weight, down_weight, residual_alpha):
        import jax, jax.numpy as jnp
        import numpy as np
        DIM = 256
        HID = 704
        E = 8
        TOP_K = 2
        EPS = 1e-06

        def _rmsnorm(x, w):
            var = jnp.mean(jnp.square(x), axis=-1, keepdims=True)
            return x * jax.lax.rsqrt(var + EPS) * w
        normed = _rmsnorm(x, norm_weight)
        logits = jnp.einsum('bsd,ed->bse', normed, router_weight)
        probs = jax.nn.softmax(logits, axis=-1)
        topk_w, topk_idx = jax.lax.top_k(probs, TOP_K)
        topk_w = topk_w / jnp.sum(topk_w, axis=-1, keepdims=True)
        combine = jnp.sum(jax.nn.one_hot(topk_idx, E, dtype=normed.dtype) * topk_w[..., None], axis=-2)
        moe_out = jnp.zeros_like(x)
        for e in range(E):
            gu = jnp.einsum('bsd,hd->bsh', normed, gate_up_weight[e])
            gate, up = (gu[..., :HID], gu[..., HID:])
            hidden = jax.nn.silu(gate) * up
            out_e = jnp.einsum('bsh,dh->bsd', hidden, down_weight[e])
            moe_out = moe_out + combine[..., e, None] * out_e
        alpha = jnp.clip(residual_alpha, -0.5, 2.0)
        return x + alpha * moe_out
    x = L0_attn_hidden_states
    xn = _layernorm(x, axis=-1)
    x = x + _L0_attn_ref(xn, L0_attn_position_embeddings, L0_attn_Wq, L0_attn_Wk, L0_attn_Wv, L0_attn_Wpost, L0_attn_Wrel, L0_attn_per_dim_scale) + _L0_ffn_ref(xn, L0_ffn_norm_weight, L0_ffn_router_weight, L0_ffn_gate_up_weight, L0_ffn_down_weight, L0_ffn_residual_alpha)
    return x

_drawn_inputs = setup_inputs


def setup_inputs(seed=0):
    import zlib

    import numpy as np

    out = dict(_drawn_inputs(seed))
    spreads = {'L0_attn_per_dim_scale': (0.0, 0.363), 'L0_ffn_norm_weight': (1.0, 0.6)}
    factors = {'L0_ffn_router_weight': 8.0, 'L0_ffn_gate_up_weight': 8.0, 'L0_ffn_down_weight': 8.0}
    for name, (base, spread) in spreads.items():
        noise = np.random.default_rng([zlib.crc32(name.encode()), seed]).standard_normal(out[name].shape)
        drawn = base * np.exp(spread * noise) if base else spread * noise
        out[name] = jnp.asarray(drawn.astype(out[name].dtype))
    for name, factor in factors.items():
        out[name] = (out[name] * factor).astype(out[name].dtype)
    return out
```

```python
from contextlib import ExitStack

import numpy as np
import concourse.bass as bass
from concourse import mybir

ALU = mybir.AluOpType
ACT = mybir.ActivationFunctionType
F32 = mybir.dt.float32
I32 = mybir.dt.int32
AX_X = mybir.AxisListType.X

P = 128
T, D = 4096, 256
KD = D // P
H, DH = 8, 32
HC = P // DH
CHUNK, PAST = 12, 12
CTX = CHUNK + PAST
NPOS = CTX + 1
SOFTCAP = 50.0
Q_SCALE = DH ** -0.5 / np.log(2.0)
K_SCALE = np.log(1.0 + np.e) / np.log(2.0)
LN_EPS, RMS_EPS = 1e-5, 1e-6

GB = 9
GQ = GB * CHUNK
NWIN = 6
GK = GQ + PAST
NG = -(-(-(-T // CHUNK)) // GB)
LASTQ = T - (NG - 1) * GQ
HV = DH + 1

E, HID = 8, 704
TT = T // P
NB = (2 * T + E * (P - 1)) // P
HALF = HID // 2
HCH = -(-HID // P)
HIDP = HCH * P
OOB = 2 * T
ALPHA_LO, ALPHA_HI = -0.5, 2.0

C_ID, C_TRI, C_ONE, C_IOTA = 0, P, 2 * P, 3 * P
C_MASK = 4 * P
C_TOK = C_MASK + GQ
C_OOB = C_TOK + TT
C_BLK = C_OOB + 1
C_EXP = C_BLK + NB
NC = C_EXP + E


def constants():
    c = np.zeros((P, NC), np.float32)
    p = np.arange(P)
    c[:, C_ID:C_ID + P] = np.eye(P)
    c[:, C_TRI:C_TRI + P] = p[:, None] < p[None, :]
    c[:, C_ONE:C_ONE + P] = 1.0
    c[:, C_IOTA:C_IOTA + P] = p[None, :]
    key = np.arange(GK)
    place = np.where(key < GQ, key, key - GK)
    ahead = place[:, None] - CHUNK * (np.arange(GQ) // CHUNK)[None, :] + PAST
    c[:GK, C_MASK:C_MASK + GQ] = (ahead >= 0) & (ahead < CTX)
    c[:, C_TOK:C_TOK + TT] = P * np.arange(TT)[None, :] + p[:, None] + 1
    c[:, C_OOB] = OOB + 1 + p
    c[:, C_BLK:C_BLK + NB] = P * np.arange(NB)[None, :]
    c[:, C_EXP:C_EXP + E] = np.arange(E)[None, :]
    return c


def program(nc, x, pos_t, wq, wk, wv, wpost, wrel, dim_scale, norm_w, router_t, gu_t, dn_t, alpha, const_d,
            xn_d, nrm_d, bd_d, out):
    with ExitStack() as ctx:
        def sb(name, shape, dt=F32):
            return ctx.enter_context(nc.sbuf_tensor(name, shape, dt))

        def sem(name):
            return ctx.enter_context(nc.semaphore(name))

        psum = ctx.enter_context(nc.psum_tensor("psum", [P, 8, 512], F32))

        gu_w = sb("gu_w", [P, E, KD, 2 * HID])
        dn_w = sb("dn_w", [P, E, HCH, D])
        const = sb("const", [P, NC])
        att_w = sb("att_w", [P, 4, KD, D])
        WQ, WK, WV, WP = range(4)
        rel_bd = sb("rel_bd", [P, KD, HC, NPOS])
        q_scale = sb("q_scale", [P, 8])
        gat_i = sb("gat_i", [P, NB], I32)
        sca_i = sb("sca_i", [P, NB], I32)
        slot_w = sb("slot_w", [P, NB])
        blk_e = sb("blk_e", [1, NB], I32)
        xg = sb("xg", [P, 3, D])

        ident = const[:, C_ID:C_ID + P]
        tri = const[:, C_TRI:C_TRI + P]
        ones = const[:, C_ONE:C_ONE + P]
        iota = const[:, C_IOTA:C_IOTA + P]
        mask = const[0:GK, C_MASK:C_MASK + GQ]

        LATE = 5
        x_all = gu_w[:, LATE:E, :, :].rearrange("p e k n -> p (e k n)")[:, 0:TT * D].rearrange(
            "p (t d) -> p t d", d=D)
        spare = dn_w[:, LATE:E, :, :].rearrange("p e k n -> p (e k) n")

        def tile8(i):
            return spare[:, i, :].rearrange("p (t e) -> p t e", e=E)

        sizes = dict(win=(NWIN + 1) * D, xres=3 * D, xnT=2 * KD * GK, qT=KD * GQ, qd=3 * H * GQ, kT=3 * KD * GK, v1=4 * H * HV,
                     bd=2 * H * NPOS, band=2 * H * GK, ex=2 * H * GQ, o=D, oT=KD * GQ, res=2 * D)
        arena = sb("arena", [P, sum(sizes.values())])
        at, off = {}, 0
        for name, n in sizes.items():
            at[name] = arena[:, off:off + n]
            off += n
        win = at["win"].rearrange("p (b d) -> p b d", b=NWIN + 1)
        xres = at["xres"].rearrange("p (b d) -> p b d", b=3)
        xnT = at["xnT"].rearrange("p (b k n) -> p b k n", b=2, k=KD)
        qT = at["qT"].rearrange("p (k n) -> p k n", k=KD)
        q_diag = at["qd"].rearrange("p (b k h n) -> p b k h n", b=3, k=KD, h=HC)
        kT = at["kT"].rearrange("p (b k n) -> p b k n", b=3, k=KD)
        v1 = at["v1"].rearrange("p (b h n) -> p b h n", b=4, h=H)
        bd = at["bd"].rearrange("p (b h n) -> p b h n", b=2, h=H)
        band = at["band"].rearrange("p (b h n) -> p b h n", b=2, h=H)
        ex = at["ex"].rearrange("p (b h n) -> p b h n", b=2, h=H)
        o_sb = at["o"].rearrange("p (h n) -> p h n", h=H)
        oT = at["oT"].rearrange("p (k n) -> p k n", k=KD)
        res = at["res"].rearrange("p (b d) -> p b d", b=2)
        fs = dict(xT=2 * KD * P, sg=2 * HID, h=2 * HIDP, hT=2 * HIDP, y=2 * D)
        at2, off = {}, 0
        for name, n in fs.items():
            at2[name] = arena[:, off:off + n]
            off += n
        xT = at2["xT"].rearrange("p (b k n) -> p b k n", b=2, k=KD)
        sg = at2["sg"].rearrange("p (b n) -> p b n", b=2)
        hb = at2["h"].rearrange("p (b n) -> p b n", b=2)
        hT = at2["hT"].rearrange("p (b k n) -> p b k n", b=2, k=HCH)
        y = at2["y"].rearrange("p (b d) -> p b d", b=2)

        mv = sb("mv", [P, TT, 2])
        st6 = spare[:, 13, 0:TT * 6].rearrange("p (t n) -> p t n", n=6)
        small = sb("small", [P, 8, TT])
        e8 = sb("e8", [P, 8, E])
        e8i = sb("e8i", [P, 2, E], I32)
        sl_i = sb("sl_i", [P, 4, TT], I32)
        al = sb("al", [P, 2])
        be = sb("be", [1, NB, E])
        bef = sb("bef", [1, NB])
        tab = sb("tab", [P, 3, NB])
        nwb = spare[:, 14, :]
        rt_w = sb("rt_w", [P, KD, E])
        wrel_s = xg[:, 0:2, :]
        pos_s = sb("pos_s", [P, KD, NPOS])
        xn_t = spare[:, 0:4, :]
        nrmT = spare[:, 4:8, :].rearrange("p a (k n) -> p a k n", k=KD)

        oh = spare[:, 15, :].rearrange("p (b n) -> p b n", b=2)
        ohb = spare[:, 16:18, :].rearrange("p a n -> p (a n)")[:, 0:4 * NB].rearrange(
            "p (b a n) -> p b a n", b=2, a=2)

        s_const = sem("s_const")
        s_small = sem("s_small")
        s_attw = sem("s_attw")
        s_x = [sem(f"s_x{i}") for i in range(4)]
        s_wexp = sem("s_wexp")
        s_st = sem("s_st")
        s_rt = sem("s_rt")
        s_sq = sem("s_sq")
        s_xn = sem("s_xn")
        s_nrm = sem("s_nrm")
        s_xnst = [sem(f"s_xnst{i}") for i in range(4)]
        s_nrmst = sem("s_nrmst")
        s_nt = sem("s_nt")
        s_nte = sem("s_nte")
        s_lg = sem("s_lg")
        s_ea = sem("s_ea")
        s_cnt = sem("s_cnt")
        s_oh = sem("s_oh")
        s_inv = sem("s_inv")
        s_tab = sem("s_tab")
        s_rel = sem("s_rel")
        s_qs = sem("s_qs")
        s_ini = sem("s_ini")
        s_win = [sem(f"s_win{i}") for i in range(NWIN + 1)]
        s_xr = [sem(f"s_xr{i}") for i in range(3)]
        s_t = sem("s_t")
        s_te = sem("s_te")
        s_q = sem("s_q")
        s_k = sem("s_k")
        s_v = sem("s_v")
        s_qe = sem("s_qe")
        s_ke = sem("s_ke")
        s_ve = sem("s_ve")
        s_bd = sem("s_bd")
        s_bde = sem("s_bde")
        s_bdw = [sem(f"s_bdw{i}") for i in range(2)]
        s_band = [sem(f"s_band{i}") for i in range(2)]
        s_s = sem("s_s")
        s_th = sem("s_th")
        s_ex = sem("s_ex")
        s_mk = sem("s_mk")
        s_pv = sem("s_pv")
        s_rc = sem("s_rc")
        s_o = sem("s_o")
        s_ot = sem("s_ot")
        s_ote = sem("s_ote")
        s_po = sem("s_po")
        s_r1 = sem("s_r1")
        s_r2 = sem("s_r2")
        s_out = [sem(f"s_out{i}") for i in range(2)]
        s_g = [sem(f"s_g{i}") for i in range(3)]
        s_xt = sem("s_xt")
        s_xte = sem("s_xte")
        s_gt = sem("s_gt")
        s_up = sem("s_up")
        s_sg = sem("s_sg")
        s_h = sem("s_h")
        s_ht = sem("s_ht")
        s_hta = sem("s_hta")
        s_htb = sem("s_htb")
        s_dn = sem("s_dn")
        s_y = sem("s_y")
        s_sc = sem("s_sc")
        s_pad = sem("s_pad")

        XCH = TT // 4

        def window(g):
            return (g % NWIN, GQ) if g < NG - 1 else (NWIN, LASTQ)

        def groups_done(eng):
            for i in range(2):
                eng.wait_ge(s_out[i], 16 * len(range(i, NG, 2)))

        block = ctx.enter_context(nc.Block())

        @block.sync
        def _(sp):
            sp.dma_start(const[:, :], const_d).then_inc(s_const, 16)
            for i in range(4):
                sp.dma_start(x_all[:, i * XCH:(i + 1) * XCH, :],
                             x[i * XCH * P:(i + 1) * XCH * P, :].rearrange("(t p) d -> p t d", p=P)).then_inc(s_x[i], 16)
            for i in range(HC):
                sp.dma_start(q_scale[DH * i:DH * (i + 1), 1:2], dim_scale).then_inc(s_small, 16)
            sp.dma_start(nwb[:, :], norm_w.to_broadcast([P, D])).then_inc(s_small, 16)
            sp.dma_start(al[:, 0:1], alpha.to_broadcast([P, 1])).then_inc(s_small, 16)
            sp.dma_start(rt_w[:, :, :], router_t.rearrange("(k p) e -> p k e", p=P)).then_inc(s_small, 16)
            sp.dma_start(pos_s[:, :, :], pos_t.rearrange("(k p) e -> p k e", p=P)).then_inc(s_small, 16)
            sp.dma_start(wrel_s, wrel.rearrange("(k p) e -> p k e", p=P)).then_inc(s_small, 16)
            for i, w in enumerate((wq, wk, wv, wpost)):
                sp.dma_start(att_w[:, i, :, :], w.rearrange("(k p) e -> p k e", p=P)).then_inc(s_attw, 16)
            for t in range(TT):
                sp.wait_ge(s_xn, t + 1)
                sp.dma_start(xn_d[t * P:(t + 1) * P, :], xn_t[:, t % 4, :]).then_inc(s_xnst[t % 4], 16)
                if t % XCH == XCH - 1:
                    i = t // XCH
                    sp.wait_ge(s_nrm, t + 1)
                    sp.dma_start(nrm_d[i * XCH * P:(i + 1) * XCH * P, :].rearrange("(t p) d -> p t d", p=P),
                                 x_all[:, i * XCH:(i + 1) * XCH, :]).then_inc(s_nrmst, 16)
            for i in range(4):
                sp.wait_ge(s_xnst[i], 16 * (TT // 4))

            def load_window(g):
                b, n = window(g)
                if g >= NWIN and b < NWIN:
                    sp.wait_ge(s_r2, g - NWIN + 1)
                sp.dma_start(win[0:n, b, :], xn_d[g * GQ:g * GQ + n, :]).then_inc(s_win[b], 16)
                if g:
                    sp.dma_start(win[GQ:GK, b, :], xn_d[g * GQ - PAST:g * GQ, :]).then_inc(s_win[b], 16)

            def load_residual(g):
                _, n = window(g)
                if g >= 3:
                    sp.wait_ge(s_r1, g - 2)
                sp.dma_start(xres[0:n, g % 3, :], x[g * GQ:g * GQ + n, :]).then_inc(s_xr[g % 3], 16)

            def shift(g):
                b = g % 2
                sp.wait_ge(s_bde, g + 1)
                sp.dma_start(bd_d[g].rearrange("h (q p) -> q h p", p=NPOS), bd[0:GQ, b, :, :]).then_inc(s_bdw[b], 16)
                sp.wait_ge(s_bdw[b], 16 * (g // 2 + 1))
                if g >= 2:
                    sp.wait_ge(s_s, g - 1)
                src = bd_d[g].rearrange("h (n f) -> n f h", n=GB)[:, 0:CHUNK * CTX, :].rearrange(
                    "n (c k) h -> n c h k", k=CTX)
                for n in range(1, GB):
                    sp.dma_start(band[CHUNK * n:CHUNK * (n + 1), b, :, CHUNK * (n - 1):CHUNK * (n + 1)],
                                 src[n]).then_inc(s_band[b], 16)
                sp.dma_start(band[0:CHUNK, b, :, GQ:GK], src[0][:, :, 0:PAST]).then_inc(s_band[b], 16)
                sp.dma_start(band[0:CHUNK, b, :, 0:CHUNK], src[0][:, :, PAST:CTX]).then_inc(s_band[b], 16)

            def expert(e):
                if e == LATE:
                    sp.wait_ge(s_tab, 4)
                    sp.wait_ge(s_nrmst, 16 * 4)
                sp.dma_start(gu_w[:, e, :, :], gu_t[e].rearrange("(k p) n -> p k n", p=P)).then_inc(s_wexp, 16)
                sp.dma_start(dn_w[:, e, 0:HCH - 1, :],
                             dn_t[e, 0:(HCH - 1) * P, :].rearrange("(k p) n -> p k n", p=P)).then_inc(s_wexp, 16)
                if e >= LATE:
                    sp.wait_ge(s_pad, 2)
                else:
                    sp.wait_ge(s_pad, 1)
                sp.dma_start(dn_w[0:HID - (HCH - 1) * P, e, HCH - 1, :],
                             dn_t[e, (HCH - 1) * P:HID, :]).then_inc(s_wexp, 16)

            sp.wait_ge(s_ini, 4)
            load_window(0)
            load_window(1)
            for s in range(NG + 4):
                if s + 2 < 5 and s + 2 < NG:
                    load_window(s + 2)
                if s < NG:
                    shift(s)
                if 0 <= s - 2 < NG:
                    load_residual(s - 2)
                if s % 3 == 1 and s // 3 < E:
                    expert(s // 3)
                if 5 <= s + 2 < NG:
                    load_window(s + 2)
                if 4 <= s:
                    g = s - 4
                    _, n = window(g)
                    sp.wait_ge(s_r2, g + 1)
                    sp.dma_start(out[g * GQ:g * GQ + n, :], res[0:n, g % 2, :]).then_inc(s_out[g % 2], 16)
            groups_done(sp)

        @block.gpsimd
        def _(pool):
            for g in range(NG):
                pool.wait_ge(s_ex, g + 1)
                pool.tensor_tensor(ex[0:GK, g % 2, :, :], ex[0:GK, g % 2, :, :],
                                   mask.rearrange("p (a n) -> p a n", a=1).to_broadcast([GK, H, GQ]),
                                   ALU.mult).then_inc(s_mk, 1)

            def gather(b):
                if b >= 3:
                    pool.wait_ge(s_xt, b - 2)
                pool.indirect_dma_start(
                    out=xg[:, b % 3, :], out_offset=None, in_=nrm_d,
                    in_offset=bass.IndirectOffsetOnAxis(ap=gat_i[:, b:b + 1], axis=0),
                    bounds_check=T - 1, oob_is_err=False).then_inc(s_g[b % 3], 16)

            def scatter(b):
                pool.wait_ge(s_y, b + 1)
                pool.wait_ge(s_sc, 16 * b)
                pool.indirect_dma_start(
                    out=out, out_offset=bass.IndirectOffsetOnAxis(ap=sca_i[:, b:b + 1], axis=0),
                    in_=y[:, b % 2, :], in_offset=None, bounds_check=T - 1, oob_is_err=False,
                    compute_op=ALU.add).then_inc(s_sc, 16)

            pool.wait_ge(s_tab, 4)
            pool.wait_ge(s_nrmst, 16 * 4)
            pool.wait_ge(s_rel, 1)
            for b in range(3):
                gather(b)
            groups_done(pool)
            for b in range(NB):
                if b + 3 < NB:
                    gather(b + 3)
                scatter(b)
            pool.wait_ge(s_sc, 16 * NB)

        @block.scalar
        def _(act):
            act.wait_ge(s_qs, 1)
            act.activation(q_scale[:, 3:4], q_scale[:, 2:3], ACT.Exp, scale=-1.0).then_inc(s_ea, 1)
            act.wait_ge(s_qs, 2)
            act.activation(q_scale[:, 5:6], q_scale[:, 4:5], ACT.Ln).then_inc(s_ea, 1)
            act.wait_ge(s_st, 1)
            act.activation(small[:, 0, :], small[:, 1, :], ACT.Sqrt).then_inc(s_sq, 1)
            act.wait_ge(s_st, 2)
            act.activation(small[:, 3, :], small[:, 4, :], ACT.Sqrt).then_inc(s_sq, 1)
            for t in range(TT):
                act.wait_ge(s_nt, t + 1)
                if t >= 4:
                    act.wait_ge(s_lg, t - 3)
                act.activation(nrmT[:, t % 4, :, :], psum[:, t % 4, 0:D].rearrange("p (k n) -> p k n", k=KD),
                               ACT.Copy).then_inc(s_nte, 1)
            act.wait_ge(s_rt, RT_EXP)
            act.activation(tile8(2), tile8(1), ACT.Exp).then_inc(s_ea, 1)

            act.wait_ge(s_qs, 3)
            for s in range(-1, NG + 4):
                if 0 <= s < NG:
                    act.wait_ge(s_q, s + 1)
                    q_ps = psum[:, 3, 0:KD * GQ].rearrange("p (k n) -> p k n", k=KD)
                    if s:
                        act.wait_ge(s_bd, s)
                    act.activation(qT[:, :, :], q_ps, ACT.Copy, scale=q_scale[:, 0:1])
                    if s == 0:
                        act.wait_ge(s_ini, 4)
                    if s >= 3:
                        act.wait_ge(s_s, s - 2)
                    for i in range(HC):
                        r = slice(DH * i, DH * (i + 1))
                        ins = act.activation(q_diag[r, s % 3, :, i, :], q_ps[r], ACT.Copy, scale=q_scale[r, 0:1])
                    ins.then_inc(s_qe, 1)
                    act.wait_ge(s_v, s + 1)
                    if s >= 4:
                        act.wait_ge(s_pv, s - 3)
                    act.activation(v1[0:GK, s % 4, :, 0:DH], psum[0:GK, 5, 0:D].rearrange("p (h n) -> p h n", h=H),
                                   ACT.Copy).then_inc(s_ve, 1)
                if 0 <= s + 1 < NG:
                    act.wait_ge(s_t, s + 2)
                    if s + 1 >= 2:
                        act.wait_ge(s_v, s)
                    act.activation(xnT[:, (s + 1) % 2, :, :],
                                   psum[:, 2, 0:KD * GK].rearrange("p (k n) -> p k n", k=KD), ACT.Copy).then_inc(s_te, 1)
                if 0 <= s - 2 < NG:
                    g = s - 2
                    act.wait_ge(s_s, g + 1)
                    sc = psum[0:GK, 0:2, 0:HC * GQ]
                    act.activation(sc, sc, ACT.Tanh, scale=1.0 / SOFTCAP).then_inc(s_th, 1)
                    act.wait_ge(s_th, g + 1)
                    if g >= 2:
                        act.wait_ge(s_pv, g - 1)
                    act.activation(ex[0:GK, g % 2, :, :].rearrange("p (a h) n -> p a (h n)", a=2), sc, ACT.Exp, scale=SOFTCAP).then_inc(s_ex, 1)

            groups_done(act)
            for b in range(-1, NB + 1):
                if 0 <= b < NB:
                    act.wait_ge(s_gt, b + 1)
                    if b >= 2:
                        act.wait_ge(s_h, b - 1)
                    act.activation(sg[:, b % 2, :].rearrange("p (a n) -> p a n", a=2), psum[:, 0:2, 0:HALF],
                                   ACT.Silu).then_inc(s_sg, 1)
                if 0 <= b - 1 < NB:
                    act.wait_ge(s_ht, b)
                    if b - 1 >= 2:
                        act.wait_ge(s_dn, b - 2)
                    act.activation(hT[:, (b - 1) % 2, 0:3, :], psum[:, 4, 0:3 * P].rearrange("p (k n) -> p k n", n=P),
                                   ACT.Copy).then_inc(s_hta, 1)
                if 0 <= b + 1 < NB:
                    act.wait_ge(s_xt, b + 2)
                    if b + 1 >= 2:
                        act.wait_ge(s_up, b)
                    act.activation(xT[:, (b + 1) % 2, :, :], psum[:, 7, 0:D].rearrange("p (k n) -> p k n", k=KD),
                                   ACT.Copy).then_inc(s_xte, 1)

        @block.vector
        def _(dve):
            chain = [0]

            def link(ins):
                chain[0] += 1
                ins.then_inc(s_rt, 1)
                dve.wait_ge(s_rt, chain[0])

            def row(i, shape):
                return small[:, i, :].rearrange("p (t a) -> p t a", a=1).to_broadcast(shape)

            S8 = [P, TT, E]
            dve.memset(band[:, :, :, :], 0.0).then_inc(s_ini, 1)
            dve.memset(v1[:, :, :, DH:HV], 1.0).then_inc(s_ini, 1)
            dve.memset(q_diag[:, :, :, :, :].rearrange("p b k h n -> p (b k h n)"), 0.0).then_inc(s_ini, 1)
            dve.memset(win[96:GK, :, :], 0.0).then_inc(s_ini, 1)
            dve.memset(dn_w[64:P, 0:LATE, HCH - 1, :], 0.0).then_inc(s_pad, 1)
            link(dve.memset(rel_bd[:, :, :, :], 0.0))
            dve.wait_ge(s_small, 16 * 9)
            link(dve.tensor_scalar(q_scale[:, 6:7], q_scale[:, 1:2], -1.0, None, ALU.mult))
            dve.tensor_tensor(q_scale[:, 2:3], q_scale[:, 1:2], q_scale[:, 6:7], ALU.max).then_inc(s_qs, 1)
            dve.wait_ge(s_ea, 1)
            dve.tensor_scalar(q_scale[:, 4:5], q_scale[:, 3:4], 1.0, None, ALU.add).then_inc(s_qs, 1)
            dve.wait_ge(s_ea, 2)
            dve.wait_ge(s_qs, 2)
            link(dve.tensor_scalar(q_scale[:, 6:7], q_scale[:, 4:5], -1.0, None, ALU.add))
            link(dve.tensor_scalar(q_scale[:, 7:8], q_scale[:, 6:7], 0.0, None, ALU.is_equal))
            link(dve.tensor_tensor(q_scale[:, 6:7], q_scale[:, 6:7], q_scale[:, 7:8], ALU.add))
            link(dve.reciprocal(q_scale[:, 6:7], q_scale[:, 6:7]))
            link(dve.scalar_tensor_tensor(out=q_scale[:, 6:7], in0=q_scale[:, 5:6], scalar=q_scale[:, 6:7],
                                          in1=q_scale[:, 7:8], op0=ALU.mult, op1=ALU.add))
            link(dve.tensor_tensor(q_scale[:, 6:7], q_scale[:, 6:7], q_scale[:, 3:4], ALU.mult))
            link(dve.scalar_tensor_tensor(out=q_scale[:, 6:7], in0=q_scale[:, 1:2], scalar=0.0,
                                          in1=q_scale[:, 6:7], op0=ALU.max, op1=ALU.add))
            dve.tensor_scalar(q_scale[:, 0:1], q_scale[:, 6:7], float(Q_SCALE), None, ALU.mult).then_inc(s_qs, 1)
            link(dve.tensor_scalar(al[:, 1:2], al[:, 0:1], ALPHA_LO, ALPHA_HI, ALU.max, ALU.min))

            dve.wait_ge(s_const, 16)
            for t in range(TT):
                if t % XCH == 0:
                    dve.wait_ge(s_x[t // XCH], 16)
                ins = dve.bn_stats(st6[:, t, :], x_all[:, t, :])
            link(ins)
            for t in range(TT):
                ins = dve.bn_aggr(mv[:, t, :], st6[:, t, :])
            link(ins)
            mean, var = mv[:, :, 0], mv[:, :, 1]
            dve.tensor_scalar(small[:, 1, :], var, LN_EPS, None, ALU.add).then_inc(s_st, 1)
            dve.wait_ge(s_sq, 1)
            link(dve.reciprocal(small[:, 2, :], small[:, 0, :]))
            link(dve.tensor_tensor(small[:, 5, :], small[:, 2, :], small[:, 2, :], ALU.mult))
            link(dve.tensor_tensor(small[:, 5, :], small[:, 5, :], var, ALU.mult))
            dve.tensor_scalar(small[:, 4, :], small[:, 5, :], RMS_EPS, None, ALU.add).then_inc(s_st, 1)
            dve.wait_ge(s_sq, 2)
            link(dve.reciprocal(small[:, 6, :], small[:, 3, :]))
            for t in range(TT):
                if t >= 4:
                    dve.wait_ge(s_xnst[t % 4], 16 * (t // 4))
                dve.tensor_scalar(xn_t[:, t % 4, :], x_all[:, t, :], mean[:, t:t + 1], small[:, 2, t:t + 1],
                                  ALU.subtract, ALU.mult).then_inc(s_xn, 1)
                dve.wait_ge(s_xn, t + 1)
                dve.scalar_tensor_tensor(out=x_all[:, t, :], in0=xn_t[:, t % 4, :], scalar=small[:, 6, t:t + 1],
                                         in1=nwb[:, :], op0=ALU.mult, op1=ALU.mult).then_inc(s_nrm, 1)
            for k in range(KD):
                dve.wait_ge(s_rel, 1)
                for i in range(HC):
                    dve.tensor_copy(rel_bd[DH * i:DH * (i + 1), k, i, :],
                                    psum[DH * i:DH * (i + 1), 6, k * NPOS:(k + 1) * NPOS]).then_inc(s_qs, 1)

            for i in range(4):
                dve.wait_ge(s_xnst[i], 16 * (TT // 4))
            dve.wait_ge(s_lg, TT)
            link(dve.tensor_copy(tile8(0), psum[:, 4, 0:TT * E].rearrange("p (t e) -> p t e", e=E)))
            link(dve.tensor_reduce(small[:, 0, :], tile8(0), AX_X, ALU.max))
            link(dve.tensor_tensor(tile8(1), tile8(0), row(0, S8), ALU.subtract))
            assert chain[0] == RT_EXP, chain[0]
            dve.wait_ge(s_ea, 3)
            link(dve.tensor_reduce(small[:, 1, :], tile8(2), AX_X, ALU.add))
            link(dve.reciprocal(small[:, 1, :], small[:, 1, :]))
            link(dve.tensor_tensor(tile8(3), tile8(2), row(1, S8), ALU.mult))
            eidx = const[:, C_EXP:C_EXP + E].rearrange("p (a e) -> p a e", a=1).to_broadcast(S8)

            def choose(prob, best, hot):
                link(dve.tensor_reduce(small[:, best, :], prob, AX_X, ALU.max))
                link(dve.tensor_tensor(tile8(8), prob, row(best, S8), ALU.is_equal))
                link(dve.scalar_tensor_tensor(out=tile8(9), in0=tile8(8), scalar=-float(E), in1=eidx,
                                              op0=ALU.mult, op1=ALU.add))
                link(dve.tensor_reduce(small[:, 7, :], tile8(9), AX_X, ALU.min))
                link(dve.tensor_scalar(small[:, 7, :], small[:, 7, :], float(E), None, ALU.add))
                link(dve.tensor_tensor(hot, eidx, row(7, S8), ALU.is_equal))

            choose(tile8(3), 0, tile8(10))
            link(dve.scalar_tensor_tensor(out=tile8(4), in0=tile8(10), scalar=-4.0, in1=tile8(3),
                                          op0=ALU.mult, op1=ALU.add))
            choose(tile8(4), 1, tile8(11))
            dve.tensor_tensor(tile8(12), tile8(10), tile8(11), ALU.add).then_inc(s_cnt, 1)
            link(dve.tensor_tensor(small[:, 2, :], small[:, 0, :], small[:, 1, :], ALU.add))
            link(dve.reciprocal(small[:, 2, :], small[:, 2, :]))
            link(dve.tensor_scalar(small[:, 2, :], small[:, 2, :], al[:, 1:2], None, ALU.mult))
            link(dve.tensor_tensor(small[:, 0, :], small[:, 0, :], small[:, 2, :], ALU.mult))
            link(dve.tensor_tensor(small[:, 1, :], small[:, 1, :], small[:, 2, :], ALU.mult))
            dve.wait_ge(s_cnt, 3)
            link(dve.tensor_copy(tile8(13), psum[:, 6, 0:TT * E].rearrange("p (t e) -> p t e", e=E)))
            for e in range(E):
                ins = dve.tensor_tensor_scan(tile8(14)[:, :, e], ones[:, 0:TT], tile8(13)[:, :, e], 0.0,
                                             ALU.mult, ALU.add)
            link(ins)
            link(dve.tensor_scalar(e8i[:, 0, :], tile8(14)[:, TT - 1, :], float(P - 1), None, ALU.add))
            link(dve.tensor_scalar(e8i[:, 1, :], e8i[:, 0, :], 7, 7, ALU.logical_shift_right, ALU.logical_shift_left))
            link(dve.tensor_copy(e8[:, 0, :], e8i[:, 1, :]))
            link(dve.tensor_tensor_scan(e8[:, 1, :], ones[:, 0:E], e8[:, 0, :], 0.0, ALU.mult, ALU.add))
            link(dve.tensor_tensor(e8[:, 2, :], e8[:, 1, :], e8[:, 0, :], ALU.subtract))
            link(dve.tensor_tensor(tile8(14), tile8(14), tile8(13), ALU.subtract))
            link(dve.tensor_tensor(tile8(14), tile8(14),
                                   e8[:, 2, :].rearrange("p (a e) -> p a e", a=1).to_broadcast(S8), ALU.add))
            link(dve.tensor_tensor(tile8(14), psum[:, 5, 0:TT * E].rearrange("p (t e) -> p t e", e=E), tile8(14),
                                   ALU.add))
            for k in range(2):
                link(dve.tensor_tensor(tile8(8), tile8(14), tile8(10 + k), ALU.mult))
                link(dve.tensor_reduce(small[:, 3, :], tile8(8), AX_X, ALU.add))
                link(dve.tensor_copy(sl_i[:, 0, :], small[:, 3, :]))
                link(dve.tensor_scalar(sl_i[:, 1, :], sl_i[:, 0, :], P - 1, None, ALU.bitwise_and))
                link(dve.tensor_scalar(sl_i[:, 2, :], sl_i[:, 0, :], 7, 7, ALU.logical_shift_right,
                                       ALU.logical_shift_left))
                link(dve.tensor_copy(small[:, 4 + k, :], sl_i[:, 1, :]))
                link(dve.tensor_copy(small[:, 6 + k, :], sl_i[:, 2, :]))
            link(dve.tensor_tensor(be[:, :, :],
                                   const[0:1, C_BLK:C_BLK + NB].rearrange("p (n a) -> p n a", a=1).to_broadcast(
                                       [1, NB, E]),
                                   e8[0:1, 1, :].rearrange("p (a e) -> p a e", a=1).to_broadcast([1, NB, E]),
                                   ALU.is_ge))
            link(dve.tensor_reduce(bef[:, :], be[:, :, :], AX_X, ALU.add))
            dve.tensor_scalar(blk_e[:, :], bef[:, :], float(E - 1), None, ALU.min).then_inc(s_tab, 1)
            blk = const[:, C_BLK:C_BLK + NB]
            for n in range(2 * TT):
                k, t = n // TT, n % TT
                if n >= 2:
                    dve.wait_ge(s_inv, n - 1)
                dve.tensor_scalar(oh[:, n % 2, :], iota, small[:, 4 + k, t:t + 1], None, ALU.is_equal)
                dve.tensor_scalar(ohb[:, n % 2, 0, :], blk, small[:, 6 + k, t:t + 1],
                                  const[:, C_TOK + t:C_TOK + t + 1], ALU.is_equal, ALU.mult)
                dve.tensor_scalar(ohb[:, n % 2, 1, :], blk, small[:, 6 + k, t:t + 1], small[:, k, t:t + 1],
                                  ALU.is_equal, ALU.mult).then_inc(s_oh, 1)
            dve.wait_ge(s_inv, 2 * TT)
            link(dve.tensor_copy(tab[:, 0, :], psum[:, 7, 0:NB]))
            dve.tensor_copy(slot_w[:, :], psum[:, 7, NB:2 * NB]).then_inc(s_tab, 1)
            link(dve.tensor_scalar(tab[:, 1, :], tab[:, 0, :], -1.0, 0.0, ALU.add, ALU.max))
            dve.tensor_copy(gat_i[:, :], tab[:, 1, :]).then_inc(s_tab, 1)
            link(dve.tensor_scalar(tab[:, 2, :], tab[:, 0, :], 0.0, const[:, C_OOB:C_OOB + 1], ALU.is_equal,
                                   ALU.mult))
            link(dve.tensor_tensor(tab[:, 2, :], tab[:, 2, :], tab[:, 0, :], ALU.add))
            dve.tensor_scalar(sca_i[:, :], tab[:, 2, :], -1.0, None, ALU.add).then_inc(s_tab, 1)
            dve.wait_ge(s_nrmst, 16 * 4)
            dve.memset(dn_w[64:P, LATE:E, HCH - 1, :], 0.0).then_inc(s_pad, 1)

            for s in range(NG + 4):
                if s < NG:
                    dve.wait_ge(s_k, s + 1)
                    if s >= 3:
                        dve.wait_ge(s_s, s - 2)
                    dve.tensor_scalar(kT[:, s % 3, :, :], psum[:, 4, 0:KD * GK].rearrange("p (k n) -> p k n", k=KD),
                                      float(K_SCALE), None, ALU.mult).then_inc(s_ke, 1)
                if 0 <= s - 3 < NG:
                    g = s - 3
                    dve.wait_ge(s_pv, g + 1)
                    pv = psum[0:GQ, 6, 0:H * HV].rearrange("p (h n) -> p h n", h=H)
                    dve.reciprocal(small[0:GQ, 0, 0:H], pv[:, :, DH:HV].rearrange("p h n -> p (h n)")).then_inc(s_rc, 1)
                    dve.wait_ge(s_rc, g + 1)
                    if g:
                        dve.wait_ge(s_ot, g)
                    dve.tensor_tensor(o_sb[0:GQ, :, :], pv[:, :, 0:DH],
                                      small[0:GQ, 0, 0:H].rearrange("p (h n) -> p h n", n=1).to_broadcast([GQ, H, DH]),
                                      ALU.mult).then_inc(s_o, 1)
                if 0 <= s - 4 < NG:
                    g = s - 4
                    wb, n = window(g)
                    dve.wait_ge(s_po, g + 1)
                    dve.wait_ge(s_xr[g % 3], 16 * (g // 3 + 1))
                    if g >= 2:
                        dve.wait_ge(s_out[g % 2], 16 * (g // 2))
                    dve.tensor_tensor(res[0:n, g % 2, :], psum[0:n, 7, 0:D], xres[0:n, g % 3, :], ALU.add).then_inc(s_r1, 1)
                    dve.wait_ge(s_r1, g + 1)
                    dve.tensor_tensor(res[0:n, g % 2, :], res[0:n, g % 2, :], win[0:n, wb, :], ALU.add).then_inc(s_r2, 1)
                if s < NG:
                    dve.wait_ge(s_bd, s + 1)
                    if s >= 2:
                        dve.wait_ge(s_bdw[s % 2], 16 * (s // 2))
                    dve.tensor_copy(bd[0:GQ, s % 2, :, :],
                                    psum[0:GQ, 4, 256:256 + H * NPOS].rearrange("p (h n) -> p h n", h=H)).then_inc(s_bde, 1)
                if 0 <= s - 3 < NG:
                    g = s - 3
                    dve.wait_ge(s_ot, g + 1)
                    if g:
                        dve.wait_ge(s_po, g)
                    dve.tensor_copy(oT[:, :, :], psum[:, 6, 0:KD * GQ].rearrange("p (k n) -> p k n", k=KD)).then_inc(s_ote, 1)

            groups_done(dve)
            for i in range(2):
                dve.memset(hb[:, i, HID:HIDP], 0.0).then_inc(s_pad, 1)
            for b in range(NB + 2):
                if b < NB:
                    dve.wait_ge(s_up, b + 1)
                    dve.wait_ge(s_sg, b + 1)
                    if b >= 2:
                        dve.wait_ge(s_ht, b - 1)
                    dve.tensor_tensor(hb[:, b % 2, 0:HID].rearrange("p (a n) -> p a n", a=2), psum[:, 2:4, 0:HALF],
                                      sg[:, b % 2, :].rearrange("p (a n) -> p a n", a=2), ALU.mult).then_inc(s_h, 1)
                if 0 <= b - 1 < NB:
                    dve.wait_ge(s_ht, b)
                    if b - 1 >= 2:
                        dve.wait_ge(s_dn, b - 2)
                    dve.tensor_copy(hT[:, (b - 1) % 2, 3:HCH, :],
                                    psum[:, 5, 0:3 * P].rearrange("p (k n) -> p k n", n=P)).then_inc(s_htb, 1)
                if 0 <= b - 2 < NB:
                    g = b - 2
                    dve.wait_ge(s_dn, g + 1)
                    if g >= 2:
                        dve.wait_ge(s_sc, 16 * (g - 1))
                    dve.tensor_scalar(y[:, g % 2, :], psum[:, 6, 0:D], slot_w[:, g:g + 1], None, ALU.mult).then_inc(s_y, 1)

        @block.tensor
        def _(pe):
            def mm(out_ap, lhs, rhs, first, last):
                return pe.matmul(out_ap, lhs, rhs, start=first, stop=last)

            pe.wait_ge(s_small, 16 * 9)
            pe.wait_ge(s_const, 16)
            for m in range(KD):
                for k in range(KD):
                    ins = mm(psum[:, 6, m * NPOS:(m + 1) * NPOS], wrel_s[:, k, m * P:(m + 1) * P], pos_s[:, k, :],
                             k == 0, k == KD - 1)
            ins.then_inc(s_rel, 1)
            for t in range(TT + 1):
                if t < TT:
                    pe.wait_ge(s_nrm, t + 1)
                    if t >= 4:
                        pe.wait_ge(s_nte, t - 3)
                    for k in range(KD):
                        ins = pe.transpose(psum[:, t % 4, k * P:(k + 1) * P], x_all[:, t, k * P:(k + 1) * P], ident)
                    ins.then_inc(s_nt, 1)
                if t >= 1:
                    u = t - 1
                    pe.wait_ge(s_nte, u + 1)
                    for k in range(KD):
                        ins = mm(psum[:, 4, u * E:(u + 1) * E], nrmT[:, u % 4, k, :], rt_w[:, k, :], k == 0, k == KD - 1)
                    ins.then_inc(s_lg, 1)
            pe.wait_ge(s_cnt, 1)
            hot = spare[:, 12, :]
            pe.wait_ge(s_qs, 3 + KD * HC)
            mm(psum[:, 5, 0:TT * E], tri, hot, True, True).then_inc(s_cnt, 1)
            mm(psum[:, 6, 0:TT * E], ones, hot, True, True).then_inc(s_cnt, 1)
            for n in range(2 * TT):
                pe.wait_ge(s_oh, n + 1)
                mm(psum[:, 7, 0:2 * NB], oh[:, n % 2, :], ohb[:, n % 2, :, :].rearrange("p a n -> p (a n)"),
                   n == 0, n == 2 * TT - 1).then_inc(s_inv, 1)

            def turn(g):
                b, _ = window(g)
                loads = sum(1 if i == 0 else 2 for i in range(g + 1) if window(i)[0] == b)
                pe.wait_ge(s_win[b], 16 * loads)
                if g:
                    pe.wait_ge(s_te, g)
                for k in range(KD):
                    ins = pe.transpose(psum[:, 2, k * GK:(k + 1) * GK], win[0:GK, b, k * P:(k + 1) * P],
                                       ident[0:GK, 0:GK])
                ins.then_inc(s_t, 1)

            pe.wait_ge(s_attw, 64)
            pe.wait_ge(s_tab, 4)
            pe.wait_ge(s_ini, 4)
            turn(0)
            for s in range(NG + 4):
                if s < NG:
                    src = xnT[:, s % 2, :, :]
                    pe.wait_ge(s_te, s + 1)
                    if s:
                        pe.wait_ge(s_qe, s)
                    for m in range(KD):
                        for k in range(KD):
                            ins = mm(psum[:, 3, m * GQ:(m + 1) * GQ], att_w[:, WQ, k, m * P:(m + 1) * P],
                                     src[:, k, 0:GQ], k == 0, k == KD - 1)
                    ins.then_inc(s_q, 1)
                    if s:
                        pe.wait_ge(s_bde, s)
                    for m in range(KD):
                        for k in range(KD):
                            ins = mm(psum[:, 4, m * GK:(m + 1) * GK], att_w[:, WK, k, m * P:(m + 1) * P],
                                     src[:, k, :], k == 0, k == KD - 1)
                    ins.then_inc(s_k, 1)
                    if s:
                        pe.wait_ge(s_ve, s)
                    for k in range(KD):
                        ins = mm(psum[0:GK, 5, 0:D], src[:, k, :], att_w[:, WV, k, :], k == 0, k == KD - 1)
                    ins.then_inc(s_v, 1)
                if s + 1 < NG:
                    turn(s + 1)
                if 0 <= s - 3 < NG:
                    g = s - 3
                    pe.wait_ge(s_mk, g + 1)
                    pe.wait_ge(s_ve, g + 1)
                    if g:
                        pe.wait_ge(s_ote, g)
                    for h in range(H):
                        ins = mm(psum[0:GQ, 6, h * HV:(h + 1) * HV], ex[0:GK, g % 2, h, :], v1[0:GK, g % 4, h, :],
                                 True, True)
                    ins.then_inc(s_pv, 1)
                if 0 <= s - 4 < NG:
                    g = s - 4
                    pe.wait_ge(s_ote, g + 1)
                    if g:
                        pe.wait_ge(s_r1, g)
                    for k in range(KD):
                        ins = mm(psum[0:GQ, 7, 0:D], oT[:, k, :], att_w[:, WP, k, :], k == 0, k == KD - 1)
                    ins.then_inc(s_po, 1)
                if s < NG:
                    pe.wait_ge(s_qe, s + 1)
                    pe.wait_ge(s_ke, s + 1)
                    for k in range(KD):
                        ins = mm(psum[0:GQ, 4, 256 + k * HC * NPOS:256 + (k + 1) * HC * NPOS], qT[:, k, :],
                                 rel_bd[:, k, :, :].rearrange("p h n -> p (h n)"), True, True)
                    ins.then_inc(s_bd, 1)
                if 0 <= s - 2 < NG:
                    g = s - 2
                    pe.wait_ge(s_band[g % 2], 160 * (g // 2 + 1))
                    if g:
                        pe.wait_ge(s_ex, g)
                    for k in range(KD):
                        mm(psum[0:GK, k, 0:HC * GQ], kT[:, g % 3, k, :],
                           q_diag[:, g % 3, k, :, :].rearrange("p h n -> p (h n)"), True, False)
                        for i in range(HC):
                            ins = mm(psum[0:GK, k, i * GQ:(i + 1) * GQ], band[0:GQ, g % 2, HC * k + i, :],
                                     ident[0:GQ, 0:GQ], False, i == HC - 1)
                    ins.then_inc(s_s, 1)
                if 0 <= s - 3 < NG:
                    g = s - 3
                    pe.wait_ge(s_o, g + 1)
                    for k in range(KD):
                        ins = pe.transpose(psum[:, 6, k * GQ:(k + 1) * GQ],
                                           o_sb[0:GQ, HC * k:HC * (k + 1), :].rearrange("p h n -> p (h n)"),
                                           ident[0:GQ, 0:GQ])
                    ins.then_inc(s_ot, 1)

            def turn_x(b):
                pe.wait_ge(s_g[b % 3], 16 * (b // 3 + 1))
                if b:
                    pe.wait_ge(s_xte, b)
                for k in range(KD):
                    ins = pe.transpose(psum[:, 7, k * P:(k + 1) * P], xg[:, b % 3, k * P:(k + 1) * P], ident)
                ins.then_inc(s_xt, 1)

            experts = [None] * NB

            def gate_up(b):
                experts[b] = pe.value_load(blk_e[0:1, b:b + 1], min_val=0, max_val=E - 1)
                pe.wait_ge(s_xte, b + 1)
                for j in range(4):
                    if b and j == 0:
                        pe.wait_ge(s_sg, b)
                    if b and j == 2:
                        pe.wait_ge(s_h, b)
                    for k in range(KD):
                        w = gu_w[:, bass.ds(experts[b], 1), k, j * HALF:(j + 1) * HALF].rearrange("p e n -> p (e n)")
                        ins = mm(psum[:, j, 0:HALF], xT[:, b % 2, k, :], w, k == 0, k == KD - 1)
                    if j == 1:
                        ins.then_inc(s_gt, 1)
                ins.then_inc(s_up, 1)

            def turn_h(b):
                pe.wait_ge(s_h, b + 1)
                if b:
                    pe.wait_ge(s_hta, b)
                    pe.wait_ge(s_htb, b)
                for c in range(HCH):
                    ins = pe.transpose(psum[:, 4 + c // 3, (c % 3) * P:(c % 3 + 1) * P], hb[:, b % 2, c * P:(c + 1) * P],
                                       ident)
                ins.then_inc(s_ht, 1)

            def down(b):
                pe.wait_ge(s_hta, b + 1)
                pe.wait_ge(s_htb, b + 1)
                if b:
                    pe.wait_ge(s_y, b)
                for c in range(HCH):
                    w = dn_w[:, bass.ds(experts[b], 1), c, :].rearrange("p e n -> p (e n)")
                    ins = mm(psum[:, 6, 0:D], hT[:, b % 2, c, :], w, c == 0, c == HCH - 1)
                ins.then_inc(s_dn, 1)

            groups_done(pe)
            pe.wait_ge(s_wexp, 48 * E)
            pe.wait_ge(s_pad, 4)
            turn_x(0)
            for b in range(NB + 2):
                if b < NB:
                    gate_up(b)
                if 0 <= b - 1 < NB:
                    turn_h(b - 1)
                if b + 1 < NB:
                    turn_x(b + 1)
                if 0 <= b - 2 < NB:
                    down(b - 2)


RT_EXP = 19


def kernel(**inputs):
    import concourse.bacc as _bacc
    from concourse.bass_utils import run_bass_kernel_spmd as _run

    def arr(name):
        return np.asarray(inputs[name])

    def turned(a, *axes):
        return np.ascontiguousarray(np.transpose(a, axes))

    arrays = {
        "x": np.ascontiguousarray(arr("L0_attn_hidden_states").reshape(T, D)),
        "pos_t": turned(arr("L0_attn_position_embeddings"), 1, 0),
        "wq": turned(arr("L0_attn_Wq"), 1, 0),
        "wk": turned(arr("L0_attn_Wk"), 1, 0),
        "wv": turned(arr("L0_attn_Wv"), 1, 0),
        "wpost": turned(arr("L0_attn_Wpost"), 1, 0),
        "wrel": turned(arr("L0_attn_Wrel"), 1, 0),
        "dim_scale": np.ascontiguousarray(arr("L0_attn_per_dim_scale").reshape(DH, 1)),
        "norm_w": np.ascontiguousarray(arr("L0_ffn_norm_weight").reshape(1, D)),
        "router_t": turned(arr("L0_ffn_router_weight"), 1, 0),
        "gu_t": turned(arr("L0_ffn_gate_up_weight"), 0, 2, 1),
        "dn_t": turned(arr("L0_ffn_down_weight"), 0, 2, 1),
        "alpha": np.ascontiguousarray(arr("L0_ffn_residual_alpha").reshape(1, 1)),
        "const": constants(),
    }
    nc = _bacc.Bacc("TRN2", target_bir_lowering=False, num_devices=1)
    args = [nc.dram_tensor("in_" + n, a.shape, mybir.dt.from_np(a.dtype), kind="ExternalInput").ap() for n, a in arrays.items()]
    args.append(nc.dram_tensor("xn_d", (T, D), F32, kind="Internal").ap())
    args.append(nc.dram_tensor("nrm_d", (T, D), F32, kind="Internal").ap())
    args.append(nc.dram_tensor("bd_d", (NG, H, GQ * NPOS), F32, kind="Internal").ap())
    args.append(nc.dram_tensor("out", (T, D), F32, kind="ExternalOutput").ap())
    program(nc, *args)
    r = _run(nc, [{"in_" + n: a for n, a in arrays.items()}], core_ids=[0])
    return r.results[0]["out"].reshape(1, T, D)
```

```python
from contextlib import ExitStack

import numpy as np
import concourse.bass as bass
from concourse import mybir

ALU = mybir.AluOpType
ACT = mybir.ActivationFunctionType
F32 = mybir.dt.float32
I32 = mybir.dt.int32
AX_X = mybir.AxisListType.X

P = 128
T, D = 4096, 256
KD = D // P
H, DH = 8, 32
HC = P // DH
CHUNK, PAST = 12, 12
CTX = CHUNK + PAST
NPOS = CTX + 1
SOFTCAP = 50.0
Q_SCALE = DH ** -0.5 / np.log(2.0)
K_SCALE = np.log(1.0 + np.e) / np.log(2.0)
LN_EPS, RMS_EPS = 1e-5, 1e-6

GB = 9
GQ = GB * CHUNK
GK = GQ + PAST
NWIN = 3
NG = -(-(-(-T // CHUNK)) // GB)
LASTT = T - (NG - 1) * GQ
NODD, NEVEN = GB // 2, GB - GB // 2
HK = GK // 2
ORDER = list(range(-1, GB, 2)) + list(range(0, GB, 2))
HV = DH + 1

E, HID = 8, 704
TT = T // P
NB = (2 * T + E * (P - 1)) // P
HALF = HID // 2
HCH = -(-HID // P)
HIDP = HCH * P
OOB = 2 * T
ALPHA_LO, ALPHA_HI = -0.5, 2.0

C_ID, C_TRI, C_ONE, C_IOTA = 0, P, 2 * P, 3 * P
C_MASK = 4 * P
C_TOK = C_MASK + GQ
C_OOB = C_TOK + TT
C_BLK = C_OOB + 1
C_EXP = C_BLK + NB
NC = C_EXP + E


def constants():
    c = np.zeros((P, NC), np.float32)
    p = np.arange(P)
    c[:, C_ID:C_ID + P] = np.eye(P)
    c[:, C_TRI:C_TRI + P] = p[:, None] < p[None, :]
    c[:, C_ONE:C_ONE + P] = 1.0
    c[:, C_IOTA:C_IOTA + P] = p[None, :]
    blk = np.repeat(ORDER, CHUNK)
    before = blk[PAST:][None, :] - blk[:, None]
    c[:GK, C_MASK:C_MASK + GQ] = (before >= 0) & (before <= 1)
    c[:, C_TOK:C_TOK + TT] = P * np.arange(TT)[None, :] + p[:, None] + 1
    c[:, C_OOB] = OOB + 1 + p
    c[:, C_BLK:C_BLK + NB] = P * np.arange(NB)[None, :]
    c[:, C_EXP:C_EXP + E] = np.arange(E)[None, :]
    return c


def program(nc, x, pos_t, wq, wk, wv, wpost, wrel, dim_scale, norm_w, router_t, gu_t, dn_t, alpha, const_d,
            xn_d, base_d, nrm_d, bd_d, out):
    with ExitStack() as ctx:
        def sb(name, shape, dt=F32):
            return ctx.enter_context(nc.sbuf_tensor(name, shape, dt))

        def sem(name):
            return ctx.enter_context(nc.semaphore(name))

        psum = ctx.enter_context(nc.psum_tensor("psum", [P, 8, 512], F32))

        gu_w = sb("gu_w", [P, E, KD, 2 * HID])
        dn_w = sb("dn_w", [P, E, HCH, D])
        const = sb("const", [P, NC])
        att_w = sb("att_w", [P, 4, KD, D])
        WQ, WK, WV, WP = range(4)
        rel_bd = sb("rel_bd", [P, KD, HC, NPOS])
        q_scale = sb("q_scale", [P, 8])
        gat_i = sb("gat_i", [P, NB], I32)
        sca_i = sb("sca_i", [P, NB], I32)
        slot_w = sb("slot_w", [P, NB])
        blk_e = sb("blk_e", [1, NB], I32)
        xg = sb("xg", [P, 3, D])

        ident = const[:, C_ID:C_ID + P]
        tri = const[:, C_TRI:C_TRI + P]
        ones = const[:, C_ONE:C_ONE + P]
        iota = const[:, C_IOTA:C_IOTA + P]
        mask = const[0:GK, C_MASK:C_MASK + GQ]

        LATE = 5
        x_all = gu_w[:, LATE:E, :, :].rearrange("p e k n -> p (e k n)")[:, 0:TT * D].rearrange(
            "p (t d) -> p t d", d=D)
        spare = dn_w[:, LATE:E, :, :].rearrange("p e k n -> p (e k) n")

        def tile8(i):
            return spare[:, i, :].rearrange("p (t e) -> p t e", e=E)

        sizes = dict(win=(NWIN + 1) * D, base=3 * D, xnT=2 * KD * GK, qT=KD * GQ, qd=3 * H * GQ, kT=3 * KD * GK, v1=4 * H * HV,
                     bd=2 * H * NPOS, shb=2 * H * CTX, rep=H * GK, ex=2 * H * GQ, o=D, oT=KD * GQ, res=2 * D)
        arena = sb("arena", [P, sum(sizes.values())])
        at, off = {}, 0
        for name, n in sizes.items():
            at[name] = arena[:, off:off + n]
            off += n
        win = at["win"].rearrange("p (b d) -> p b d", b=NWIN + 1)
        base = at["base"].rearrange("p (b d) -> p b d", b=3)
        xnT = at["xnT"].rearrange("p (b k n) -> p b k n", b=2, k=KD)
        qT = at["qT"].rearrange("p (k n) -> p k n", k=KD)
        q_diag = at["qd"].rearrange("p (b k h n) -> p b k h n", b=3, k=KD, h=HC)
        kT = at["kT"].rearrange("p (b k n) -> p b k n", b=3, k=KD)
        v1 = at["v1"].rearrange("p (b h n) -> p b h n", b=4, h=H)
        bd = at["bd"].rearrange("p (b n h) -> p b n h", b=2, h=H)
        spread = at["rep"].rearrange("p (h a r n) -> p h a r n", h=H, a=2, n=CHUNK)
        shifted = at["shb"].rearrange("p (b a n h) -> p b a n h", b=2, h=H, a=2)
        ex = at["ex"].rearrange("p (b h n) -> p b h n", b=2, h=H)
        o_sb = at["o"].rearrange("p (h n) -> p h n", h=H)
        oT = at["oT"].rearrange("p (k n) -> p k n", k=KD)
        res = at["res"].rearrange("p (b d) -> p b d", b=2)
        fs = dict(xT=2 * KD * P, sg=2 * HID, h=2 * HIDP, hT=2 * HIDP, y=2 * D)
        at2, off = {}, 0
        for name, n in fs.items():
            at2[name] = arena[:, off:off + n]
            off += n
        xT = at2["xT"].rearrange("p (b k n) -> p b k n", b=2, k=KD)
        sg = at2["sg"].rearrange("p (b n) -> p b n", b=2)
        hb = at2["h"].rearrange("p (b n) -> p b n", b=2)
        hT = at2["hT"].rearrange("p (b k n) -> p b k n", b=2, k=HCH)
        y = at2["y"].rearrange("p (b d) -> p b d", b=2)

        mv = sb("mv", [P, TT, 2])
        st6 = spare[:, 13, 0:TT * 6].rearrange("p (t n) -> p t n", n=6)
        small = sb("small", [P, 8, TT])
        e8 = sb("e8", [P, 8, E])
        e8i = sb("e8i", [P, 2, E], I32)
        sl_i = sb("sl_i", [P, 4, TT], I32)
        al = sb("al", [P, 2])
        be = sb("be", [1, NB, E])
        bef = sb("bef", [1, NB])
        rden = sb("rden", [P, H])
        tab = sb("tab", [P, 3, NB])
        nwb = spare[:, 14, :]
        rt_w = sb("rt_w", [P, KD, E])
        wrel_s = xg[:, 0:2, :]
        pos_s = sb("pos_s", [P, KD, NPOS])
        xn_t = spare[:, 0:4, :]
        base_t = spare[:, 4:8, :]
        nrmT = spare[:, 8:10, :].rearrange("p a (k n) -> p a k n", k=KD)
        NOH = 6
        oh_all = spare[:, 0:8, :].rearrange("p a n -> p (a n)")[:, 0:NOH * (P + 2 * NB)].rearrange(
            "p (b n) -> p b n", b=NOH)
        oh = oh_all[:, :, 0:P]
        ohb = oh_all[:, :, P:P + 2 * NB].rearrange("p b (a n) -> p b a n", a=2)

        s_const = sem("s_const")
        s_small = sem("s_small")
        s_attw = sem("s_attw")
        s_x = [sem(f"s_x{i}") for i in range(4)]
        s_wexp = sem("s_wexp")
        s_st = sem("s_st")
        s_rt = sem("s_rt")
        s_sq = sem("s_sq")
        s_xn = sem("s_xn")
        s_nrm = sem("s_nrm")
        s_n1 = sem("s_n1")
        s_ra = sem("s_ra")
        s_xnst = [sem(f"s_xnst{i}") for i in range(2)]
        s_bs = sem("s_bs")
        s_bsst = [sem(f"s_bsst{i}") for i in range(2)]
        s_nrmst = sem("s_nrmst")
        s_nt = sem("s_nt")
        s_nte = sem("s_nte")
        s_lg = sem("s_lg")
        s_ea = sem("s_ea")
        s_cnt = sem("s_cnt")
        s_oh = sem("s_oh")
        s_inv = sem("s_inv")
        s_tab = sem("s_tab")
        s_rel = sem("s_rel")
        s_qs = sem("s_qs")
        s_ini = sem("s_ini")
        s_win = [sem(f"s_win{i}") for i in range(NWIN + 1)]
        s_xr = [sem(f"s_xr{i}") for i in range(3)]
        s_t = sem("s_t")
        s_te = sem("s_te")
        s_q = sem("s_q")
        s_k = sem("s_k")
        s_v = sem("s_v")
        s_qe = sem("s_qe")
        s_ke = sem("s_ke")
        s_ve = sem("s_ve")
        s_bd = sem("s_bd")
        s_bde = sem("s_bde")
        s_bdw = [sem(f"s_bdw{i}") for i in range(2)]
        s_band = [sem(f"s_band{i}") for i in range(2)]
        s_s = sem("s_s")
        s_th = sem("s_th")
        s_ex = sem("s_ex")
        s_mk = sem("s_mk")
        s_pv = sem("s_pv")
        s_rc = sem("s_rc")
        s_rep = sem("s_rep")
        s_o = sem("s_o")
        s_ot = sem("s_ot")
        s_ote = sem("s_ote")
        s_po = sem("s_po")
        s_r2 = sem("s_r2")
        s_out = [sem(f"s_out{i}") for i in range(2)]
        s_g = [sem(f"s_g{i}") for i in range(3)]
        s_xt = sem("s_xt")
        s_xte = sem("s_xte")
        s_gt = sem("s_gt")
        s_up = sem("s_up")
        s_sg = sem("s_sg")
        s_h = sem("s_h")
        s_ht = sem("s_ht")
        s_hta = sem("s_hta")
        s_htb = sem("s_htb")
        s_dn = sem("s_dn")
        s_y = sem("s_y")
        s_sc = sem("s_sc")
        s_pad = sem("s_pad")

        TPS = 3
        S_A = -(-TT // TPS) + 1
        S_HOT = S_A + 3
        S_OH = S_HOT + 4
        OPS = 5
        S_TAB = S_OH + -(-2 * TT // OPS)

        XCH = TT // 4

        def window(g):
            return g % NWIN if g < NG - 1 else NWIN

        def query_rows(dram, g):
            t0 = g * GQ
            if g < NG - 1:
                odd = dram[t0:t0 + 2 * NODD * CHUNK, :].rearrange("(i a c) d -> i a c d", a=2, c=CHUNK)[:, 1]
                even = dram[t0 - PAST:t0 + GQ, :] if g else None
                if g:
                    even = even.rearrange("(i a c) d -> i a c d", a=2, c=CHUNK)[:, 1]
                    return [(odd, 0, NODD * CHUNK), (even, NODD * CHUNK, NEVEN * CHUNK)]
            pairs = (min(GQ, T - t0)) // (2 * CHUNK)
            both = dram[t0:t0 + pairs * 2 * CHUNK, :].rearrange("(i a c) d -> i a c d", a=2, c=CHUNK)
            tail = dram[t0 + pairs * 2 * CHUNK:min(t0 + GQ, T), :]
            return [(both[:, 1], 0, pairs * CHUNK), (both[:, 0], NODD * CHUNK, pairs * CHUNK),
                    (tail, (NODD + pairs) * CHUNK, tail.shape[0])]

        def stores(g, b):
            return sum(len(query_rows(out, i)) for i in range(g + 1) if i % 2 == b)

        def groups_done(eng):
            for i in range(2):
                eng.wait_ge(s_out[i], 16 * stores(NG - 1, i))

        block = ctx.enter_context(nc.Block())

        @block.sync
        def _(sp):
            s_done = [0]
            sp.dma_start(const[:, :], const_d).then_inc(s_const, 16)
            for i in range(4):
                sp.dma_start(x_all[:, i * XCH:(i + 1) * XCH, :],
                             x[i * XCH * P:(i + 1) * XCH * P, :].rearrange("(t p) d -> p t d", p=P)).then_inc(s_x[i], 16)
            for i in range(HC):
                sp.dma_start(q_scale[DH * i:DH * (i + 1), 1:2], dim_scale).then_inc(s_small, 16)
            sp.dma_start(nwb[:, :], norm_w.to_broadcast([P, D])).then_inc(s_small, 16)
            sp.dma_start(al[:, 0:1], alpha.to_broadcast([P, 1])).then_inc(s_small, 16)
            sp.dma_start(rt_w[:, :, :], router_t.rearrange("(k p) e -> p k e", p=P)).then_inc(s_small, 16)
            sp.dma_start(pos_s[:, :, :], pos_t.rearrange("(k p) e -> p k e", p=P)).then_inc(s_small, 16)
            sp.dma_start(wrel_s, wrel.rearrange("(k p) e -> p k e", p=P)).then_inc(s_small, 16)
            for i, w in enumerate((wq, wk, wv, wpost)):
                sp.dma_start(att_w[:, i, :, :], w.rearrange("(k p) e -> p k e", p=P)).then_inc(s_attw, 16)
            for t in range(1, TT, 2):
                rows = slice((t - 1) * P, (t + 1) * P)
                b = t // 2 % 2
                sp.wait_ge(s_xn, t + 1)
                sp.dma_start(xn_d[rows, :].rearrange("(t p) d -> p t d", p=P),
                             xn_t[:, 2 * b:2 * b + 2, :]).then_inc(s_xnst[b], 16)
                sp.wait_ge(s_bs, t + 1)
                sp.dma_start(base_d[rows, :].rearrange("(t p) d -> p t d", p=P),
                             base_t[:, 2 * b:2 * b + 2, :]).then_inc(s_bsst[b], 16)

            def store_normed(i):
                sp.wait_ge(s_nrm, (i + 1) * XCH)
                sp.dma_start(nrm_d[i * XCH * P:(i + 1) * XCH * P, :].rearrange("(t p) d -> p t d", p=P),
                             x_all[:, i * XCH:(i + 1) * XCH, :]).then_inc(s_nrmst, 16)

            def load_window(g):
                b = window(g)
                if g >= NWIN and b < NWIN:
                    sp.wait_ge(s_t, g - NWIN + 1)
                t0 = g * GQ - PAST
                if 0 < g < NG - 1:
                    src = xn_d[t0:t0 + GK, :].rearrange("(i a c) d -> a i c d", a=2, c=CHUNK)
                    for a in range(2):
                        sp.dma_start(win[a * HK:(a + 1) * HK, b, :], src[a]).then_inc(s_win[b], 16)
                    return
                for src, row, n in query_rows(xn_d, g):
                    sp.dma_start(win[PAST + row:PAST + row + n, b, :], src).then_inc(s_win[b], 16)
                if g:
                    sp.dma_start(win[0:PAST, b, :], xn_d[t0:t0 + PAST, :]).then_inc(s_win[b], 16)

            def load_base(g):
                if g >= 3:
                    sp.wait_ge(s_r2, g - 2)
                for src, row, n in query_rows(base_d, g):
                    sp.dma_start(base[row:row + n, g % 3, :], src).then_inc(s_xr[g % 3], 16)

            def flat_out(g):
                sp.wait_ge(s_bde, g + 1)
                sp.dma_start(bd_d[g], bd[0:GQ, g % 2, :, :].rearrange("q n h -> q (n h)")).then_inc(s_bdw[g % 2], 16)

            def shift_in(g):
                b = g % 2
                sp.wait_ge(s_bdw[b], 16 * (g // 2 + 1))
                if g >= 2:
                    sp.wait_ge(s_rep, g - 1)
                src = bd_d[g].rearrange("(n c) f -> n (c f)", c=CHUNK)[:, 0:CHUNK * CTX * H].rearrange(
                    "n (c f) -> n c f", c=CHUNK)
                r, half = NODD * CHUNK, PAST * H
                dst = shifted[:, b, :, :, :].rearrange("q a n h -> q (a n h)")
                sp.dma_start(dst[0:r, 0:half], src[0:NODD, :, half:2 * half]).then_inc(s_band[b], 16)
                sp.dma_start(dst[0:r, half:2 * half], src[0:NODD, :, 0:half]).then_inc(s_band[b], 16)
                sp.dma_start(dst[r:GQ, :], src[NODD:GB]).then_inc(s_band[b], 16)

            def expert(e):
                if e == LATE:
                    sp.wait_ge(s_tab, 4)
                    sp.wait_ge(s_nrmst, 16 * 4)
                sp.dma_start(gu_w[:, e, :, :], gu_t[e].rearrange("(k p) n -> p k n", p=P)).then_inc(s_wexp, 16)
                sp.dma_start(dn_w[:, e, 0:HCH - 1, :],
                             dn_t[e, 0:(HCH - 1) * P, :].rearrange("(k p) n -> p k n", p=P)).then_inc(s_wexp, 16)
                if e >= LATE:
                    sp.wait_ge(s_pad, 2)
                else:
                    sp.wait_ge(s_pad, 1)
                sp.dma_start(dn_w[0:HID - (HCH - 1) * P, e, HCH - 1, :],
                             dn_t[e, (HCH - 1) * P:HID, :]).then_inc(s_wexp, 16)

            for i in range(2):
                sp.wait_ge(s_xnst[i], 16 * (TT // 4))
                sp.wait_ge(s_bsst[i], 16 * (TT // 4))
            sp.wait_ge(s_ini, 4)
            for g in range(NWIN):
                load_window(g)
            load_base(0)
            for s in range(NG + 4):
                if s < NG:
                    flat_out(s)
                if NWIN <= s + 2 < NG:
                    load_window(s + 2)
                if 4 <= s:
                    g = s - 4
                    sp.wait_ge(s_r2, g + 1)
                    for dst, row, n in query_rows(out, g):
                        sp.dma_start(dst, res[row:row + n, g % 2, :]).then_inc(s_out[g % 2], 16)
                if 1 <= s - 1 < NG:
                    load_base(s - 1)
                if s < NG:
                    shift_in(s)
                if s >= 1 and s * TPS >= XCH * (s_done[0] + 1) and s_done[0] < 4:
                    store_normed(s_done[0])
                    s_done[0] += 1
                if s % 3 == 1 and s // 3 < LATE:
                    expert(s // 3)
                if s == S_TAB + 1:
                    for e in range(LATE, E):
                        expert(e)
            groups_done(sp)

        @block.gpsimd
        def _(pool):
            for t in range(TT):
                pool.wait_ge(s_xn, t + 1)
                if t >= 4:
                    pool.wait_ge(s_bsst[t // 2 % 2], 16 * (t // 4))
                pool.tensor_tensor(base_t[:, t % 4, :], x_all[:, t, :], xn_t[:, t % 4, :], ALU.add).then_inc(s_bs, 1)
            for g in range(NG):
                pool.wait_ge(s_ex, g + 1)
                pool.tensor_tensor(ex[0:GK, g % 2, :, :], ex[0:GK, g % 2, :, :],
                                   mask.rearrange("p (a n) -> p a n", a=1).to_broadcast([GK, H, GQ]),
                                   ALU.mult).then_inc(s_mk, 1)

            def gather(b):
                if b >= 3:
                    pool.wait_ge(s_xt, b - 2)
                pool.indirect_dma_start(
                    out=xg[:, b % 3, :], out_offset=None, in_=nrm_d,
                    in_offset=bass.IndirectOffsetOnAxis(ap=gat_i[:, b:b + 1], axis=0),
                    bounds_check=T - 1, oob_is_err=False).then_inc(s_g[b % 3], 16)

            def scatter(b):
                pool.wait_ge(s_y, b + 1)
                pool.wait_ge(s_sc, 16 * b)
                pool.indirect_dma_start(
                    out=out, out_offset=bass.IndirectOffsetOnAxis(ap=sca_i[:, b:b + 1], axis=0),
                    in_=y[:, b % 2, :], in_offset=None, bounds_check=T - 1, oob_is_err=False,
                    compute_op=ALU.add).then_inc(s_sc, 16)

            pool.wait_ge(s_tab, 4)
            pool.wait_ge(s_nrmst, 16 * 4)
            pool.wait_ge(s_rel, 1)
            for b in range(3):
                gather(b)
            groups_done(pool)
            for b in range(NB):
                if b + 3 < NB:
                    gather(b + 3)
                scatter(b)
            pool.wait_ge(s_sc, 16 * NB)

        @block.scalar
        def _(act):
            act.wait_ge(s_qs, 1)
            act.activation(q_scale[:, 3:4], q_scale[:, 2:3], ACT.Exp, scale=-1.0).then_inc(s_ea, 1)
            act.wait_ge(s_qs, 2)
            act.activation(q_scale[:, 5:6], q_scale[:, 4:5], ACT.Ln).then_inc(s_ea, 1)
            act.wait_ge(s_st, 1)
            act.activation(small[:, 0, :], small[:, 1, :], ACT.Sqrt).then_inc(s_sq, 1)
            act.wait_ge(s_st, 2)
            act.activation(small[:, 3, :], small[:, 4, :], ACT.Sqrt).then_inc(s_sq, 1)

            def normed_evac(t):
                if t < TT:
                    act.wait_ge(s_nt, t + 1)
                    if t >= 2:
                        act.wait_ge(s_lg, t - 1)
                    act.activation(nrmT[:, t % 2, :, :], psum[:, 3, D:2 * D].rearrange("p (k n) -> p k n", k=KD),
                                   ACT.Copy).then_inc(s_nte, 1)

            act.wait_ge(s_qs, 3)
            for s in range(-1, NG + 4):
                tile = TPS * (s - 1) if 1 <= s < S_A else TT
                if s == S_A + 1:
                    act.wait_ge(s_ra, 1)
                    act.activation(tile8(2), tile8(1), ACT.Exp).then_inc(s_ea, 1)
                if 0 <= s < NG:
                    act.wait_ge(s_q, s + 1)
                    q_ps = psum[:, 2, D:D + KD * GQ].rearrange("p (k n) -> p k n", k=KD)
                    if s:
                        act.wait_ge(s_bd, s)
                    act.activation(qT[:, :, :], q_ps, ACT.Copy, scale=q_scale[:, 0:1])
                    if s == 0:
                        act.wait_ge(s_ini, 4)
                    if s >= 3:
                        act.wait_ge(s_s, s - 2)
                    for i in range(HC):
                        r = slice(DH * i, DH * (i + 1))
                        ins = act.activation(q_diag[r, s % 3, :, i, :], q_ps[r], ACT.Copy, scale=q_scale[r, 0:1])
                    ins.then_inc(s_qe, 1)
                    act.wait_ge(s_v, s + 1)
                    if s >= 4:
                        act.wait_ge(s_pv, s - 3)
                    act.activation(v1[0:GK, s % 4, :, 0:DH], psum[0:GK, 5, 0:D].rearrange("p (h n) -> p h n", h=H),
                                   ACT.Copy).then_inc(s_ve, 1)
                normed_evac(tile)
                if 0 <= s + 1 < NG:
                    act.wait_ge(s_t, s + 2)
                    if s + 1 >= 2:
                        act.wait_ge(s_v, s)
                    act.activation(xnT[:, (s + 1) % 2, :, :],
                                   psum[:, 2, 0:KD * GK].rearrange("p (k n) -> p k n", k=KD), ACT.Copy).then_inc(s_te, 1)
                normed_evac(tile + 1)
                if 0 <= s - 2 < NG:
                    g = s - 2
                    act.wait_ge(s_s, g + 1)
                    sc = psum[0:GK, 0:2, 0:HC * GQ]
                    act.activation(sc, sc, ACT.Tanh, scale=1.0 / SOFTCAP).then_inc(s_th, 1)
                    act.wait_ge(s_th, g + 1)
                    if g >= 2:
                        act.wait_ge(s_pv, g - 1)
                    act.activation(ex[0:GK, g % 2, :, :].rearrange("p (a h) n -> p a (h n)", a=2), sc, ACT.Exp, scale=SOFTCAP).then_inc(s_ex, 1)
                normed_evac(tile + 2)

            groups_done(act)
            for b in range(-1, NB + 1):
                if 0 <= b < NB:
                    act.wait_ge(s_gt, b + 1)
                    if b >= 2:
                        act.wait_ge(s_h, b - 1)
                    act.activation(sg[:, b % 2, :].rearrange("p (a n) -> p a n", a=2), psum[:, 0:2, 0:HALF],
                                   ACT.Silu).then_inc(s_sg, 1)
                if 0 <= b - 1 < NB:
                    act.wait_ge(s_ht, b)
                    if b - 1 >= 2:
                        act.wait_ge(s_dn, b - 2)
                    act.activation(hT[:, (b - 1) % 2, 0:3, :], psum[:, 4, 0:3 * P].rearrange("p (k n) -> p k n", n=P),
                                   ACT.Copy).then_inc(s_hta, 1)
                if 0 <= b + 1 < NB:
                    act.wait_ge(s_xt, b + 2)
                    if b + 1 >= 2:
                        act.wait_ge(s_up, b)
                    act.activation(xT[:, (b + 1) % 2, :, :], psum[:, 7, 0:D].rearrange("p (k n) -> p k n", k=KD),
                                   ACT.Copy).then_inc(s_xte, 1)

        @block.vector
        def _(dve):
            chain = [0]

            def link(ins):
                chain[0] += 1
                ins.then_inc(s_rt, 1)
                dve.wait_ge(s_rt, chain[0])

            def row(i, shape):
                return small[:, i, :].rearrange("p (t a) -> p t a", a=1).to_broadcast(shape)

            S8 = [P, TT, E]
            dve.memset(v1[:, :, :, DH:HV], 1.0).then_inc(s_ini, 1)
            dve.memset(q_diag[:, :, :, :, :].rearrange("p b k h n -> p (b k h n)"), 0.0).then_inc(s_ini, 1)
            dve.memset(win[:, 0, :], 0.0).then_inc(s_ini, 1)
            dve.memset(win[:, NWIN, :], 0.0).then_inc(s_ini, 1)
            dve.memset(dn_w[64:P, 0:LATE, HCH - 1, :], 0.0).then_inc(s_pad, 1)
            link(dve.memset(rel_bd[:, :, :, :], 0.0))
            dve.wait_ge(s_small, 16 * 9)
            link(dve.tensor_scalar(q_scale[:, 6:7], q_scale[:, 1:2], -1.0, None, ALU.mult))
            dve.tensor_tensor(q_scale[:, 2:3], q_scale[:, 1:2], q_scale[:, 6:7], ALU.max).then_inc(s_qs, 1)
            dve.wait_ge(s_ea, 1)
            dve.tensor_scalar(q_scale[:, 4:5], q_scale[:, 3:4], 1.0, None, ALU.add).then_inc(s_qs, 1)
            dve.wait_ge(s_ea, 2)
            dve.wait_ge(s_qs, 2)
            link(dve.tensor_scalar(q_scale[:, 6:7], q_scale[:, 4:5], -1.0, None, ALU.add))
            link(dve.tensor_scalar(q_scale[:, 7:8], q_scale[:, 6:7], 0.0, None, ALU.is_equal))
            link(dve.tensor_tensor(q_scale[:, 6:7], q_scale[:, 6:7], q_scale[:, 7:8], ALU.add))
            link(dve.reciprocal(q_scale[:, 6:7], q_scale[:, 6:7]))
            link(dve.scalar_tensor_tensor(out=q_scale[:, 6:7], in0=q_scale[:, 5:6], scalar=q_scale[:, 6:7],
                                          in1=q_scale[:, 7:8], op0=ALU.mult, op1=ALU.add))
            link(dve.tensor_tensor(q_scale[:, 6:7], q_scale[:, 6:7], q_scale[:, 3:4], ALU.mult))
            link(dve.scalar_tensor_tensor(out=q_scale[:, 6:7], in0=q_scale[:, 1:2], scalar=0.0,
                                          in1=q_scale[:, 6:7], op0=ALU.max, op1=ALU.add))
            dve.tensor_scalar(q_scale[:, 0:1], q_scale[:, 6:7], float(Q_SCALE), None, ALU.mult).then_inc(s_qs, 1)
            link(dve.tensor_scalar(al[:, 1:2], al[:, 0:1], ALPHA_LO, ALPHA_HI, ALU.max, ALU.min))

            dve.wait_ge(s_const, 16)
            for t in range(TT):
                if t % XCH == 0:
                    dve.wait_ge(s_x[t // XCH], 16)
                ins = dve.bn_stats(st6[:, t, :], x_all[:, t, :])
            link(ins)
            for t in range(TT):
                ins = dve.bn_aggr(mv[:, t, :], st6[:, t, :])
            link(ins)
            mean, var = mv[:, :, 0], mv[:, :, 1]
            dve.tensor_scalar(small[:, 1, :], var, LN_EPS, None, ALU.add).then_inc(s_st, 1)
            dve.wait_ge(s_sq, 1)
            link(dve.reciprocal(small[:, 2, :], small[:, 0, :]))
            link(dve.tensor_tensor(small[:, 5, :], small[:, 2, :], small[:, 2, :], ALU.mult))
            link(dve.tensor_tensor(small[:, 5, :], small[:, 5, :], var, ALU.mult))
            dve.tensor_scalar(small[:, 4, :], small[:, 5, :], RMS_EPS, None, ALU.add).then_inc(s_st, 1)
            dve.wait_ge(s_sq, 2)
            link(dve.reciprocal(small[:, 6, :], small[:, 3, :]))
            link(dve.tensor_tensor(small[:, 6, :], small[:, 6, :], small[:, 2, :], ALU.mult))
            for t in range(TT):
                if t >= 4:
                    dve.wait_ge(s_xnst[t // 2 % 2], 16 * (t // 4))
                    dve.wait_ge(s_bs, t - 3)
                dve.tensor_scalar(xn_t[:, t % 4, :], x_all[:, t, :], mean[:, t:t + 1], small[:, 2, t:t + 1],
                                  ALU.subtract, ALU.mult).then_inc(s_xn, 1)

            def normed(t):
                dve.wait_ge(s_bs, t + 1)
                dve.tensor_scalar(x_all[:, t, :], x_all[:, t, :], mean[:, t:t + 1], small[:, 6, t:t + 1],
                                  ALU.subtract, ALU.mult).then_inc(s_n1, 1)
                dve.wait_ge(s_n1, t + 1)
                dve.tensor_tensor(x_all[:, t, :], x_all[:, t, :], nwb, ALU.mult).then_inc(s_nrm, 1)

            for k in range(KD):
                dve.wait_ge(s_rel, 1)
                for i in range(HC):
                    dve.tensor_copy(rel_bd[DH * i:DH * (i + 1), k, i, :],
                                    psum[DH * i:DH * (i + 1), 6, k * NPOS:(k + 1) * NPOS]).then_inc(s_qs, 1)

            def routing():
                for i in range(2):
                    dve.wait_ge(s_xnst[i], 16 * (TT // 4))
                    dve.wait_ge(s_bsst[i], 16 * (TT // 4))
                dve.wait_ge(s_lg, TT)
                link(dve.tensor_copy(tile8(0), psum[:, 3, 0:TT * E].rearrange("p (t e) -> p t e", e=E)))
                link(dve.tensor_reduce(small[:, 0, :], tile8(0), AX_X, ALU.max))
                dve.tensor_tensor(tile8(1), tile8(0), row(0, S8), ALU.subtract).then_inc(s_ra, 1)
                yield
                dve.wait_ge(s_ea, 3)
                link(dve.tensor_reduce(small[:, 1, :], tile8(2), AX_X, ALU.add))
                link(dve.reciprocal(small[:, 1, :], small[:, 1, :]))
                link(dve.tensor_tensor(tile8(3), tile8(2), row(1, S8), ALU.mult))
                eidx = const[:, C_EXP:C_EXP + E].rearrange("p (a e) -> p a e", a=1).to_broadcast(S8)

                def choose(prob, best, hot):
                    link(dve.tensor_reduce(small[:, best, :], prob, AX_X, ALU.max))
                    link(dve.tensor_tensor(tile8(8), prob, row(best, S8), ALU.is_equal))
                    link(dve.scalar_tensor_tensor(out=tile8(9), in0=tile8(8), scalar=-float(E), in1=eidx,
                                                  op0=ALU.mult, op1=ALU.add))
                    link(dve.tensor_reduce(small[:, 7, :], tile8(9), AX_X, ALU.min))
                    link(dve.tensor_scalar(small[:, 7, :], small[:, 7, :], float(E), None, ALU.add))
                    link(dve.tensor_tensor(hot, eidx, row(7, S8), ALU.is_equal))

                choose(tile8(3), 0, tile8(10))
                yield
                link(dve.scalar_tensor_tensor(out=tile8(4), in0=tile8(10), scalar=-4.0, in1=tile8(3),
                                              op0=ALU.mult, op1=ALU.add))
                choose(tile8(4), 1, tile8(11))
                dve.tensor_tensor(tile8(12), tile8(10), tile8(11), ALU.add).then_inc(s_cnt, 1)
                yield
                link(dve.tensor_tensor(small[:, 2, :], small[:, 0, :], small[:, 1, :], ALU.add))
                link(dve.reciprocal(small[:, 2, :], small[:, 2, :]))
                link(dve.tensor_scalar(small[:, 2, :], small[:, 2, :], al[:, 1:2], None, ALU.mult))
                link(dve.tensor_tensor(small[:, 0, :], small[:, 0, :], small[:, 2, :], ALU.mult))
                link(dve.tensor_tensor(small[:, 1, :], small[:, 1, :], small[:, 2, :], ALU.mult))
                dve.wait_ge(s_cnt, 3)
                link(dve.tensor_copy(tile8(13), psum[:, 3, TT * E:2 * TT * E].rearrange("p (t e) -> p t e", e=E)))
                for e in range(E):
                    ins = dve.tensor_tensor_scan(tile8(14)[:, :, e], ones[:, 0:TT], tile8(13)[:, :, e], 0.0,
                                                 ALU.mult, ALU.add)
                link(ins)
                yield
                link(dve.tensor_scalar(e8i[:, 0, :], tile8(14)[:, TT - 1, :], float(P - 1), None, ALU.add))
                link(dve.tensor_scalar(e8i[:, 1, :], e8i[:, 0, :], 7, 7, ALU.logical_shift_right, ALU.logical_shift_left))
                link(dve.tensor_copy(e8[:, 0, :], e8i[:, 1, :]))
                link(dve.tensor_tensor_scan(e8[:, 1, :], ones[:, 0:E], e8[:, 0, :], 0.0, ALU.mult, ALU.add))
                link(dve.tensor_tensor(e8[:, 2, :], e8[:, 1, :], e8[:, 0, :], ALU.subtract))
                link(dve.tensor_tensor(tile8(14), tile8(14), tile8(13), ALU.subtract))
                link(dve.tensor_tensor(tile8(14), tile8(14),
                                       e8[:, 2, :].rearrange("p (a e) -> p a e", a=1).to_broadcast(S8), ALU.add))
                link(dve.tensor_tensor(tile8(14), psum[:, 3, 0:TT * E].rearrange("p (t e) -> p t e", e=E), tile8(14),
                                       ALU.add))
                for k in range(2):
                    yield
                    link(dve.tensor_tensor(tile8(8), tile8(14), tile8(10 + k), ALU.mult))
                    link(dve.tensor_reduce(small[:, 3, :], tile8(8), AX_X, ALU.add))
                    link(dve.tensor_copy(sl_i[:, 0, :], small[:, 3, :]))
                    link(dve.tensor_scalar(sl_i[:, 1, :], sl_i[:, 0, :], P - 1, None, ALU.bitwise_and))
                    link(dve.tensor_scalar(sl_i[:, 2, :], sl_i[:, 0, :], 7, 7, ALU.logical_shift_right,
                                           ALU.logical_shift_left))
                    link(dve.tensor_copy(small[:, 4 + k, :], sl_i[:, 1, :]))
                    link(dve.tensor_copy(small[:, 6 + k, :], sl_i[:, 2, :]))
                link(dve.tensor_tensor(be[:, :, :],
                                       const[0:1, C_BLK:C_BLK + NB].rearrange("p (n a) -> p n a", a=1).to_broadcast(
                                           [1, NB, E]),
                                       e8[0:1, 1, :].rearrange("p (a e) -> p a e", a=1).to_broadcast([1, NB, E]),
                                       ALU.is_ge))
                link(dve.tensor_reduce(bef[:, :], be[:, :, :], AX_X, ALU.add))
                dve.tensor_scalar(blk_e[:, :], bef[:, :], float(E - 1), None, ALU.min).then_inc(s_tab, 1)
                blk = const[:, C_BLK:C_BLK + NB]
                for n in range(2 * TT):
                    if n % OPS == 0:
                        yield
                    k, t = n // TT, n % TT
                    if n >= NOH:
                        dve.wait_ge(s_inv, n - NOH + 1)
                    dve.tensor_scalar(oh[:, n % NOH, :], iota, small[:, 4 + k, t:t + 1], None, ALU.is_equal)
                    dve.tensor_scalar(ohb[:, n % NOH, 0, :], blk, small[:, 6 + k, t:t + 1],
                                      const[:, C_TOK + t:C_TOK + t + 1], ALU.is_equal, ALU.mult)
                    dve.tensor_scalar(ohb[:, n % NOH, 1, :], blk, small[:, 6 + k, t:t + 1], small[:, k, t:t + 1],
                                      ALU.is_equal, ALU.mult).then_inc(s_oh, 1)
                yield
                dve.wait_ge(s_inv, 2 * TT)
                link(dve.tensor_copy(tab[:, 0, :], psum[:, 3, 0:NB]))
                dve.tensor_copy(slot_w[:, :], psum[:, 3, NB:2 * NB]).then_inc(s_tab, 1)
                link(dve.tensor_scalar(tab[:, 1, :], tab[:, 0, :], -1.0, 0.0, ALU.add, ALU.max))
                dve.tensor_copy(gat_i[:, :], tab[:, 1, :]).then_inc(s_tab, 1)
                link(dve.tensor_scalar(tab[:, 2, :], tab[:, 0, :], 0.0, const[:, C_OOB:C_OOB + 1], ALU.is_equal,
                                       ALU.mult))
                link(dve.tensor_tensor(tab[:, 2, :], tab[:, 2, :], tab[:, 0, :], ALU.add))
                dve.tensor_scalar(sca_i[:, :], tab[:, 2, :], -1.0, None, ALU.add).then_inc(s_tab, 1)
                dve.wait_ge(s_nrmst, 16 * 4)
                dve.memset(dn_w[64:P, LATE:E, HCH - 1, :], 0.0).then_inc(s_pad, 1)
                yield

            route = routing()
            steps = [S_A, S_A + 1, S_A + 2, S_HOT, S_HOT + 1, S_HOT + 2, S_HOT + 3]
            steps += list(range(S_OH, S_TAB + 1))

            for s in range(NG + 4):
                for t in range(TPS * s, min(TPS * (s + 1), TT)):
                    normed(t)
                if s in steps:
                    next(route)
                if 0 <= s - 2 < NG:
                    g = s - 2
                    dve.wait_ge(s_band[g % 2], 48 * (g // 2 + 1))
                    if g:
                        dve.wait_ge(s_s, g)
                    for a in range(2):
                        rel = shifted[0:GQ, g % 2, a, :, :].rearrange("p (r n) h -> p h r n", r=1)
                        ins = dve.tensor_copy(spread[0:GQ, :, a, :, :],
                                              rel.to_broadcast([GQ, H, HK // CHUNK, CHUNK]))
                    ins.then_inc(s_rep, 1)
                if s < NG:
                    dve.wait_ge(s_k, s + 1)
                    if s >= 3:
                        dve.wait_ge(s_s, s - 2)
                    dve.tensor_scalar(kT[:, s % 3, :, :], psum[:, 4, 0:KD * GK].rearrange("p (k n) -> p k n", k=KD),
                                      float(K_SCALE), None, ALU.mult).then_inc(s_ke, 1)
                if 0 <= s - 3 < NG:
                    g = s - 3
                    dve.wait_ge(s_pv, g + 1)
                    pv = psum[0:GQ, 6, 0:H * HV].rearrange("p (h n) -> p h n", h=H)
                    dve.reciprocal(rden[0:GQ, :], pv[:, :, DH:HV].rearrange("p h n -> p (h n)")).then_inc(s_rc, 1)
                    dve.wait_ge(s_rc, g + 1)
                    if g:
                        dve.wait_ge(s_ot, g)
                    dve.tensor_tensor(o_sb[0:GQ, :, :], pv[:, :, 0:DH],
                                      rden[0:GQ, :].rearrange("p (h n) -> p h n", n=1).to_broadcast([GQ, H, DH]),
                                      ALU.mult).then_inc(s_o, 1)
                if 0 <= s - 4 < NG:
                    g = s - 4
                    loads = sum(len(query_rows(base_d, i)) for i in range(g + 1) if i % 3 == g % 3)
                    dve.wait_ge(s_po, g + 1)
                    dve.wait_ge(s_xr[g % 3], 16 * loads)
                    if g >= 2:
                        dve.wait_ge(s_out[g % 2], 16 * stores(g - 2, g % 2))
                    dve.tensor_tensor(res[0:GQ, g % 2, :], psum[0:GQ, 7, 0:D], base[0:GQ, g % 3, :],
                                      ALU.add).then_inc(s_r2, 1)
                if s < NG:
                    dve.wait_ge(s_bd, s + 1)
                    if s >= 2:
                        dve.wait_ge(s_bdw[s % 2], 16 * (s // 2))
                    dve.tensor_copy(bd[0:GQ, s % 2, :, :],
                                    psum[0:GQ, 4, D:D + H * NPOS].rearrange("p (h n) -> p n h", h=H)).then_inc(s_bde, 1)
                if 0 <= s - 3 < NG:
                    g = s - 3
                    dve.wait_ge(s_ot, g + 1)
                    if g:
                        dve.wait_ge(s_po, g)
                    dve.tensor_copy(oT[:, :, :], psum[:, 6, 0:KD * GQ].rearrange("p (k n) -> p k n", k=KD)).then_inc(s_ote, 1)

            groups_done(dve)
            for i in range(2):
                dve.memset(hb[:, i, HID:HIDP], 0.0).then_inc(s_pad, 1)
            for b in range(NB + 2):
                if b < NB:
                    dve.wait_ge(s_up, b + 1)
                    dve.wait_ge(s_sg, b + 1)
                    if b >= 2:
                        dve.wait_ge(s_ht, b - 1)
                    dve.tensor_tensor(hb[:, b % 2, 0:HID].rearrange("p (a n) -> p a n", a=2), psum[:, 2:4, 0:HALF],
                                      sg[:, b % 2, :].rearrange("p (a n) -> p a n", a=2), ALU.mult).then_inc(s_h, 1)
                if 0 <= b - 1 < NB:
                    dve.wait_ge(s_ht, b)
                    if b - 1 >= 2:
                        dve.wait_ge(s_dn, b - 2)
                    dve.tensor_copy(hT[:, (b - 1) % 2, 3:HCH, :],
                                    psum[:, 5, 0:3 * P].rearrange("p (k n) -> p k n", n=P)).then_inc(s_htb, 1)
                if 0 <= b - 2 < NB:
                    g = b - 2
                    dve.wait_ge(s_dn, g + 1)
                    if g >= 2:
                        dve.wait_ge(s_sc, 16 * (g - 1))
                    dve.tensor_scalar(y[:, g % 2, :], psum[:, 6, 0:D], slot_w[:, g:g + 1], None, ALU.mult).then_inc(s_y, 1)

        @block.tensor
        def _(pe):
            def mm(out_ap, lhs, rhs, first, last):
                return pe.matmul(out_ap, lhs, rhs, start=first, stop=last)

            pe.wait_ge(s_small, 16 * 9)
            pe.wait_ge(s_const, 16)
            for m in range(KD):
                for k in range(KD):
                    ins = mm(psum[:, 6, m * NPOS:(m + 1) * NPOS], wrel_s[:, k, m * P:(m + 1) * P], pos_s[:, k, :],
                             k == 0, k == KD - 1)
            ins.then_inc(s_rel, 1)

            def logits(t):
                if 1 <= t <= TT:
                    u = t - 1
                    pe.wait_ge(s_nte, u + 1)
                    for k in range(KD):
                        ins = mm(psum[:, 3, u * E:(u + 1) * E], nrmT[:, u % 2, k, :], rt_w[:, k, :], k == 0, k == KD - 1)
                    ins.then_inc(s_lg, 1)
                if t < TT:
                    pe.wait_ge(s_nrm, t + 1)
                    for k in range(KD):
                        ins = pe.transpose(psum[:, 3, D + k * P:D + (k + 1) * P], x_all[:, t, k * P:(k + 1) * P], ident)
                    ins.then_inc(s_nt, 1)

            def count():
                pe.wait_ge(s_cnt, 1)
                hot = spare[:, 12, :]
                mm(psum[:, 3, 0:TT * E], tri, hot, True, True).then_inc(s_cnt, 1)
                mm(psum[:, 3, TT * E:2 * TT * E], ones, hot, True, True).then_inc(s_cnt, 1)

            def tables(first, last):
                for n in range(first, min(last, 2 * TT)):
                    pe.wait_ge(s_oh, n + 1)
                    mm(psum[:, 3, 0:2 * NB], oh[:, n % NOH, :], ohb[:, n % NOH, :, :].rearrange("p a n -> p (a n)"),
                       n == 0, n == 2 * TT - 1).then_inc(s_inv, 1)

            def turn(g):
                b = window(g)
                loads = sum(len(query_rows(xn_d, i)) + (i > 0) if i in (0, NG - 1) else 2
                            for i in range(g + 1) if window(i) == b)
                pe.wait_ge(s_win[b], 16 * loads)
                if g:
                    pe.wait_ge(s_qe, g)
                for k in range(KD):
                    ins = pe.transpose(psum[:, 2, k * GK:(k + 1) * GK], win[0:GK, b, k * P:(k + 1) * P],
                                       ident[0:GK, 0:GK])
                ins.then_inc(s_t, 1)

            pe.wait_ge(s_attw, 64)
            pe.wait_ge(s_qs, 3 + KD * HC)
            pe.wait_ge(s_ini, 4)
            turn(0)
            for s in range(NG + 4):
                tile = TPS * (s - 1) if 1 <= s <= S_A else TT + 1
                if s == S_HOT:
                    count()
                if s > S_OH:
                    tables(OPS * (s - S_OH - 1), OPS * (s - S_OH))
                if s < NG:
                    src = xnT[:, s % 2, :, :]
                    pe.wait_ge(s_te, s + 1)
                    if s:
                        pe.wait_ge(s_qe, s)
                    for m in range(KD):
                        for k in range(KD):
                            ins = mm(psum[:, 2, D + m * GQ:D + (m + 1) * GQ], att_w[:, WQ, k, m * P:(m + 1) * P],
                                     src[:, k, PAST:GK], k == 0, k == KD - 1)
                    ins.then_inc(s_q, 1)
                    if s:
                        pe.wait_ge(s_bde, s)
                    for m in range(KD):
                        for k in range(KD):
                            ins = mm(psum[:, 4, m * GK:(m + 1) * GK], att_w[:, WK, k, m * P:(m + 1) * P],
                                     src[:, k, :], k == 0, k == KD - 1)
                    ins.then_inc(s_k, 1)
                    if s:
                        pe.wait_ge(s_ve, s)
                    for k in range(KD):
                        ins = mm(psum[0:GK, 5, 0:D], src[:, k, :], att_w[:, WV, k, :], k == 0, k == KD - 1)
                    ins.then_inc(s_v, 1)
                logits(tile)
                if s + 1 < NG:
                    turn(s + 1)
                if 0 <= s - 3 < NG:
                    g = s - 3
                    pe.wait_ge(s_mk, g + 1)
                    pe.wait_ge(s_ve, g + 1)
                    if g:
                        pe.wait_ge(s_ote, g)
                    for h in range(H):
                        ins = mm(psum[0:GQ, 6, h * HV:(h + 1) * HV], ex[0:GK, g % 2, h, :], v1[0:GK, g % 4, h, :],
                                 True, True)
                    ins.then_inc(s_pv, 1)
                if 0 <= s - 4 < NG:
                    g = s - 4
                    pe.wait_ge(s_ote, g + 1)
                    if g:
                        pe.wait_ge(s_r2, g)
                    for k in range(KD):
                        ins = mm(psum[0:GQ, 7, 0:D], oT[:, k, :], att_w[:, WP, k, :], k == 0, k == KD - 1)
                    ins.then_inc(s_po, 1)
                logits(tile + 1)
                if s < NG:
                    pe.wait_ge(s_qe, s + 1)
                    pe.wait_ge(s_ke, s + 1)
                    for k in range(KD):
                        ins = mm(psum[0:GQ, 4, 256 + k * HC * NPOS:256 + (k + 1) * HC * NPOS], qT[:, k, :],
                                 rel_bd[:, k, :, :].rearrange("p h n -> p (h n)"), True, True)
                    ins.then_inc(s_bd, 1)
                if 0 <= s - 2 < NG:
                    g = s - 2
                    pe.wait_ge(s_rep, g + 1)
                    if g:
                        pe.wait_ge(s_ex, g)
                    for k in range(KD):
                        for i in range(HC):
                            pe.matmul(psum[0:GK, k, i * GQ:(i + 1) * GQ],
                                      spread[0:GQ, HC * k + i, :, :, :].rearrange("p a r n -> p (a r n)"),
                                      ident[0:GQ, 0:GQ], start=i == 0, stop=False, is_transpose=True)
                        ins = mm(psum[0:GK, k, 0:HC * GQ], kT[:, g % 3, k, :],
                                 q_diag[:, g % 3, k, :, :].rearrange("p h n -> p (h n)"), False, True)
                    ins.then_inc(s_s, 1)
                logits(tile + 2)
                if 0 <= s - 3 < NG:
                    g = s - 3
                    pe.wait_ge(s_o, g + 1)
                    for k in range(KD):
                        ins = pe.transpose(psum[:, 6, k * GQ:(k + 1) * GQ],
                                           o_sb[0:GQ, HC * k:HC * (k + 1), :].rearrange("p h n -> p (h n)"),
                                           ident[0:GQ, 0:GQ])
                    ins.then_inc(s_ot, 1)

            def turn_x(b):
                pe.wait_ge(s_g[b % 3], 16 * (b // 3 + 1))
                if b:
                    pe.wait_ge(s_xte, b)
                for k in range(KD):
                    ins = pe.transpose(psum[:, 7, k * P:(k + 1) * P], xg[:, b % 3, k * P:(k + 1) * P], ident)
                ins.then_inc(s_xt, 1)

            experts = [None] * NB

            def gate_up(b):
                experts[b] = pe.value_load(blk_e[0:1, b:b + 1], min_val=0, max_val=E - 1)
                pe.wait_ge(s_xte, b + 1)
                for j in range(4):
                    if b and j == 0:
                        pe.wait_ge(s_sg, b)
                    if b and j == 2:
                        pe.wait_ge(s_h, b)
                    for k in range(KD):
                        w = gu_w[:, bass.ds(experts[b], 1), k, j * HALF:(j + 1) * HALF].rearrange("p e n -> p (e n)")
                        ins = mm(psum[:, j, 0:HALF], xT[:, b % 2, k, :], w, k == 0, k == KD - 1)
                    if j == 1:
                        ins.then_inc(s_gt, 1)
                ins.then_inc(s_up, 1)

            def turn_h(b):
                pe.wait_ge(s_h, b + 1)
                if b:
                    pe.wait_ge(s_hta, b)
                    pe.wait_ge(s_htb, b)
                for c in range(HCH):
                    ins = pe.transpose(psum[:, 4 + c // 3, (c % 3) * P:(c % 3 + 1) * P], hb[:, b % 2, c * P:(c + 1) * P],
                                       ident)
                ins.then_inc(s_ht, 1)

            def down(b):
                pe.wait_ge(s_hta, b + 1)
                pe.wait_ge(s_htb, b + 1)
                if b:
                    pe.wait_ge(s_y, b)
                for c in range(HCH):
                    w = dn_w[:, bass.ds(experts[b], 1), c, :].rearrange("p e n -> p (e n)")
                    ins = mm(psum[:, 6, 0:D], hT[:, b % 2, c, :], w, c == 0, c == HCH - 1)
                ins.then_inc(s_dn, 1)

            groups_done(pe)
            pe.wait_ge(s_wexp, 48 * E)
            pe.wait_ge(s_pad, 4)
            turn_x(0)
            for b in range(NB + 2):
                if b < NB:
                    gate_up(b)
                if 0 <= b - 1 < NB:
                    turn_h(b - 1)
                if b + 1 < NB:
                    turn_x(b + 1)
                if 0 <= b - 2 < NB:
                    down(b - 2)


RT_EXP = 19


def kernel(**inputs):
    import concourse.bacc as _bacc
    from concourse.bass_utils import run_bass_kernel_spmd as _run

    def arr(name):
        return np.asarray(inputs[name])

    def turned(a, *axes):
        return np.ascontiguousarray(np.transpose(a, axes))

    arrays = {
        "x": np.ascontiguousarray(arr("L0_attn_hidden_states").reshape(T, D)),
        "pos_t": turned(arr("L0_attn_position_embeddings"), 1, 0),
        "wq": turned(arr("L0_attn_Wq"), 1, 0),
        "wk": turned(arr("L0_attn_Wk"), 1, 0),
        "wv": turned(arr("L0_attn_Wv"), 1, 0),
        "wpost": turned(arr("L0_attn_Wpost"), 1, 0),
        "wrel": turned(arr("L0_attn_Wrel"), 1, 0),
        "dim_scale": np.ascontiguousarray(arr("L0_attn_per_dim_scale").reshape(DH, 1)),
        "norm_w": np.ascontiguousarray(arr("L0_ffn_norm_weight").reshape(1, D)),
        "router_t": turned(arr("L0_ffn_router_weight"), 1, 0),
        "gu_t": turned(arr("L0_ffn_gate_up_weight"), 0, 2, 1),
        "dn_t": turned(arr("L0_ffn_down_weight"), 0, 2, 1),
        "alpha": np.ascontiguousarray(arr("L0_ffn_residual_alpha").reshape(1, 1)),
        "const": constants(),
    }
    nc = _bacc.Bacc("TRN2", target_bir_lowering=False, num_devices=1)
    args = [nc.dram_tensor("in_" + n, a.shape, mybir.dt.from_np(a.dtype), kind="ExternalInput").ap() for n, a in arrays.items()]
    args.append(nc.dram_tensor("xn_d", (T, D), F32, kind="Internal").ap())
    args.append(nc.dram_tensor("base_d", (T, D), F32, kind="Internal").ap())
    args.append(nc.dram_tensor("nrm_d", (T, D), F32, kind="Internal").ap())
    args.append(nc.dram_tensor("bd_d", (NG, GQ, NPOS * H), F32, kind="Internal").ap())
    args.append(nc.dram_tensor("out", (T, D), F32, kind="ExternalOutput").ap())
    program(nc, *args)
    r = _run(nc, [{"in_" + n: a for n, a in arrays.items()}], core_ids=[0])
    return r.results[0]["out"].reshape(1, T, D)
```

```python
from contextlib import ExitStack

import numpy as np
import concourse.bass as bass
from concourse import mybir

ALU = mybir.AluOpType
ACT = mybir.ActivationFunctionType
F32 = mybir.dt.float32
F32R = mybir.dt.float32r
I32 = mybir.dt.int32
AX_X = mybir.AxisListType.X

P = 128
T, D = 4096, 256
KD = D // P
H, DH = 8, 32
HM = 5
HC = P // DH
CHUNK, PAST = 12, 12
CTX = CHUNK + PAST
NPOS = CTX + 1
SOFTCAP = 50.0
Q_SCALE = DH ** -0.5 / np.log(2.0)
K_SCALE = np.log(1.0 + np.e) / np.log(2.0)
LN_EPS, RMS_EPS = 1e-5, 1e-6

GB = 9
GQ = GB * CHUNK
GK = GQ + PAST
NWIN = 3
NG = -(-(-(-T // CHUNK)) // GB)
LASTT = T - (NG - 1) * GQ
NODD, NEVEN = GB // 2, GB - GB // 2
HK = GK // 2
ORDER = list(range(-1, GB, 2)) + list(range(0, GB, 2))
HV = DH + 1

E, HID = 8, 704
TT = T // P
NB = (2 * T + E * (P - 1)) // P
NB_MIN = 2 * T // P
HALF = HID // 2
HCH = -(-HID // P)
HIDP = HCH * P
GU_COLS = KD * 2 * HID
WC = GU_COLS + HCH * D
NRING = 3
HI, LO = 0, 1
PASSES = ((HI, HI), (HI, LO), (LO, HI))
REST = HID - (HCH - 1) * P
NPC = 4
PC = WC // NPC
NST = 4
NXG = 5
LPE = 2 * NPC
PCS = 2 * NPC
OOB = 2 * T
ALPHA_LO, ALPHA_HI = -0.5, 2.0

C_ID, C_TRI, C_ONE, C_IOTA = 0, P, 2 * P, 3 * P
C_MASK = 4 * P
C_TOK = C_MASK + GQ
C_OOB = C_TOK + TT
C_BLK = C_OOB + 1
C_EXP = C_BLK + NB
NC = C_EXP + E


def constants():
    c = np.zeros((P, NC), np.float32)
    p = np.arange(P)
    c[:, C_ID:C_ID + P] = np.eye(P)
    c[:, C_TRI:C_TRI + P] = p[:, None] < p[None, :]
    c[:, C_ONE:C_ONE + P] = 1.0
    c[:, C_IOTA:C_IOTA + P] = p[None, :]
    blk = np.repeat(ORDER, CHUNK)
    before = blk[PAST:][None, :] - blk[:, None]
    c[:GK, C_MASK:C_MASK + GQ] = (before >= 0) & (before <= 1)
    c[:, C_TOK:C_TOK + TT] = P * np.arange(TT)[None, :] + p[:, None] + 1
    c[:, C_OOB] = OOB + 1 + p
    c[:, C_BLK:C_BLK + NB] = P * np.arange(NB)[None, :]
    c[:, C_EXP:C_EXP + E] = np.arange(E)[None, :]
    return c


def program(nc, x, pos_t, wq, wk, wv, wpost, wrel, dim_scale, norm_w, router_t, w_raw, alpha, const_d,
            xn_d, base_d, nrm_d, bd_d, w_split, out):
    with ExitStack() as ctx:
        cursor = [-(-nc.sbuf_base // 32) * 32]

        def sb(name, shape, dt=F32, at=None):
            n = 4 * int(np.prod(shape[1:]))
            if at is None:
                at = cursor[0]
                cursor[0] += -(-n // 32) * 32
            return nc.alloc_sbuf_tensor_at(name, shape, dt, offset=at)

        def sem(name):
            return ctx.enter_context(nc.semaphore(name))

        psum = ctx.enter_context(nc.psum_tensor("psum", [P, 8, 512], F32))

        const = sb("const", [P, NC])
        att_w = sb("att_w", [P, 2, KD, D])
        WQ, WK = range(2)
        vp_w = sb("vp_w", [P, 2, 2, KD, D], F32R)
        WV, WP = range(2)
        rel_bd = sb("rel_bd", [P, KD, HC, NPOS])
        q_scale = sb("q_scale", [P, 8])
        gat_i = sb("gat_i", [P, NB], I32)
        sca_i = sb("sca_i", [P, NB], I32)
        slot_w = sb("slot_w", [P, NB])
        blk_slot = sb("blk_slot", [1, NB], I32)
        blk_load = sb("blk_load", [1, NB], I32)
        first_blk = sb("first_blk", [1, E], I32)
        in_use = sb("in_use", [1, 2], I32)
        xg = sb("xg", [P, NXG, D])

        ident = const[:, C_ID:C_ID + P]
        tri = const[:, C_TRI:C_TRI + P]
        ones = const[:, C_ONE:C_ONE + P]
        iota = const[:, C_IOTA:C_IOTA + P]
        mask = const[0:GK, C_MASK:C_MASK + GQ]

        ring_at = cursor[0]
        w_ring = sb("w_ring", [P, NRING, 2, WC], F32R)
        raw_at = cursor[0]
        raw = sb("raw", [P, NST, PC])
        vp_raw = sb("vp_raw", [P, 2, KD, D], at=raw_at)
        xn_all = sb("xn_all", [P, TT, D], at=ring_at)
        base_all = sb("base_all", [P, TT, D], at=ring_at + 2 * WC * 4)
        x_all = sb("x_all", [P, TT, D], at=ring_at + 2 * 2 * WC * 4)

        spare = sb("spare", [P, 15, D])

        def tile8(i):
            return spare[:, i, :].rearrange("p (t e) -> p t e", e=E)

        sizes = dict(win=(NWIN + 1) * D, xnT=2 * KD * GK, qT=KD * GQ, qd=3 * H * GQ, kT=3 * KD * GK, bd=2 * H * NPOS,
                     shb=2 * H * CTX, rep=H * GK, between=776, v1=4 * H * HV, ex=2 * H * GQ, base=3 * D, o=D, oT=KD * GQ,
                     res=2 * D)
        arena_at = cursor[0]
        arena = sb("arena", [P, sum(sizes.values())])
        at, off = {}, 0
        for name, n in sizes.items():
            at[name] = arena[:, off:off + n]
            off += n
        win = at["win"].rearrange("p (b d) -> p b d", b=NWIN + 1)
        base = at["base"].rearrange("p (b d) -> p b d", b=3)
        xnT = at["xnT"].rearrange("p (b k n) -> p b k n", b=2, k=KD)
        qT = at["qT"].rearrange("p (k n) -> p k n", k=KD)
        q_diag = at["qd"].rearrange("p (b k h n) -> p b k h n", b=3, k=KD, h=HC)
        kT = at["kT"].rearrange("p (b k n) -> p b k n", b=3, k=KD)
        v1 = at["v1"].rearrange("p (b h n) -> p b h n", b=4, h=H)
        bd = at["bd"].rearrange("p (b n h) -> p b n h", b=2, h=H)
        spread = at["rep"].rearrange("p (h a r n) -> p h a r n", h=H, a=2, n=CHUNK)
        shifted = at["shb"].rearrange("p (b a n h) -> p b a n h", b=2, h=H, a=2)
        ex = at["ex"].rearrange("p (b h n) -> p b h n", b=2, h=H)
        o_sb = at["o"].rearrange("p (h n) -> p h n", h=H)

        def place(name, before=0):
            return arena_at + 4 * (sum(list(sizes.values())[:list(sizes).index(name)]) + before)

        oT_hi = sb("oT_hi", [P, KD, GQ], F32R, at=place("oT"))
        xv = sb("xv", [P, 2, KD, GK], F32R, at=place("between"))
        oT_lo = sb("oT_lo", [P, KD, GQ], F32R, at=place("between", 2 * KD * GK))
        res = at["res"].rearrange("p (b d) -> p b d", b=2)
        fcur = [arena_at]

        def ffn(name, shape, dt=F32):
            at = fcur[0]
            fcur[0] += 4 * int(np.prod(shape[1:]))
            return sb(name, shape, dt, at=at)

        xT = ffn("xT", [P, 2, 2, KD, P], F32R)
        hT = ffn("hT", [P, 2, 2, HCH, P], F32R)
        sg = ffn("sg", [P, 2, HID])
        hb = ffn("hb", [P, 2, HIDP])
        y = ffn("y", [P, 2, D])
        assert fcur[0] <= arena_at + 4 * sum(list(sizes.values())[:list(sizes).index("v1")])

        mv = sb("mv", [P, TT, 2])
        st6 = spare[:, 13, 0:TT * 6].rearrange("p (t n) -> p t n", n=6)
        small = sb("small", [P, 8, TT])
        e8 = sb("e8", [P, 8, E])
        e8i = sb("e8i", [P, 3, E], I32)
        sl_i = sb("sl_i", [P, 4, TT], I32)
        al = sb("al", [P, 2])
        be = spare[0:1, 0:3, :].rearrange("p a n -> p (a n)")[:, 0:NB * E].rearrange("p (n e) -> p n e", e=E)
        bef = sb("bef", [1, 4, NB])
        rden = sb("rden", [P, H])
        tab = spare[:, 13, 0:3 * NB].rearrange("p (a n) -> p a n", n=NB)
        nwb = spare[:, 14, :]
        rt_w = sb("rt_w", [P, KD, E])
        wrel_s = xg[:, 0:2, :]
        pos_s = xg[:, 2, 0:KD * NPOS].rearrange("p (k n) -> p k n", k=KD)
        nrmT = spare[:, 8:10, :].rearrange("p a (k n) -> p a k n", k=KD)
        NOH = 6
        oh_all = spare[:, 0:8, :].rearrange("p a n -> p (a n)")[:, 0:NOH * (P + 2 * NB)].rearrange(
            "p (b n) -> p b n", b=NOH)
        oh = oh_all[:, :, 0:P]
        ohb = oh_all[:, :, P:P + 2 * NB].rearrange("p b (a n) -> p b a n", a=2)

        s_const = sem("s_const")
        s_dim = sem("s_dim")
        s_small = sem("s_small")
        s_attw = sem("s_attw")
        s_vpw = sem("s_vpw")
        s_vph = sem("s_vph")
        s_vpl = sem("s_vpl")
        s_xvl = sem("s_xvl")
        s_oth = sem("s_oth")
        s_x = [sem(f"s_x{i}") for i in range(5)]
        s_raw = [sem(f"s_raw{i}") for i in range(NST)]
        s_hi = sem("s_hi")
        s_spl = sem("s_spl")
        s_wst = [sem(f"s_wst{i}") for i in range(PCS)]
        s_w = sem("s_w")
        s_st = sem("s_st")
        s_rt = sem("s_rt")
        s_sq = sem("s_sq")
        s_xn = sem("s_xn")
        s_nrm = sem("s_nrm")
        s_n1 = sem("s_n1")
        s_ra = sem("s_ra")
        s_xnst = [sem(f"s_xnst{i}") for i in range(5)]
        s_bs = sem("s_bs")
        s_bsst = [sem(f"s_bsst{i}") for i in range(5)]
        s_nrmst = sem("s_nrmst")
        s_nt = sem("s_nt")
        s_nte = sem("s_nte")
        s_lg = sem("s_lg")
        s_ea = sem("s_ea")
        s_cnt = sem("s_cnt")
        s_oh = sem("s_oh")
        s_inv = sem("s_inv")
        s_tab = sem("s_tab")
        s_rel = sem("s_rel")
        s_qs = sem("s_qs")
        s_ini = sem("s_ini")
        s_win = [sem(f"s_win{i}") for i in range(NWIN + 1)]
        s_xr = [sem(f"s_xr{i}") for i in range(3)]
        s_t = sem("s_t")
        s_te = sem("s_te")
        s_q = sem("s_q")
        s_k = sem("s_k")
        s_v = sem("s_v")
        s_qe = sem("s_qe")
        s_ke = sem("s_ke")
        s_ve = sem("s_ve")
        s_bd = sem("s_bd")
        s_bde = sem("s_bde")
        s_bdw = [sem(f"s_bdw{i}") for i in range(2)]
        s_band = [sem(f"s_band{i}") for i in range(2)]
        s_s = sem("s_s")
        s_th = sem("s_th")
        s_ex = sem("s_ex")
        s_mk = sem("s_mk")
        s_mkd = sem("s_mkd")
        s_pv = sem("s_pv")
        s_rc = sem("s_rc")
        s_rep = sem("s_rep")
        s_o = sem("s_o")
        s_ot = sem("s_ot")
        s_ote = sem("s_ote")
        s_po = sem("s_po")
        s_r2 = sem("s_r2")
        s_out = [sem(f"s_out{i}") for i in range(2)]
        s_g = [sem(f"s_g{i}") for i in range(NXG)]
        s_xt = sem("s_xt")
        s_xte = sem("s_xte")
        s_xtl = sem("s_xtl")
        s_gt = sem("s_gt")
        s_up = sem("s_up")
        s_sg = sem("s_sg")
        s_h = sem("s_h")
        s_ht = sem("s_ht")
        s_hta = sem("s_hta")
        s_htb = sem("s_htb")
        s_htl = sem("s_htl")
        s_dn = sem("s_dn")
        s_y = sem("s_y")
        s_sc = sem("s_sc")

        TPS = 3
        S_A = -(-TT // TPS) + 1
        S_HOT = S_A + 3
        S_OH = S_HOT + 4
        OPS = 5
        S_TAB = S_OH + -(-2 * TT // OPS)

        XCH = TT // 4
        X0 = XCH // 2
        PARTS = [(0, X0), (X0, XCH)] + [(i * XCH, (i + 1) * XCH) for i in range(1, TT // XCH)]
        NRT = 2

        def window(g):
            return g % NWIN if g < NG - 1 else NWIN

        def query_rows(dram, g):
            t0 = g * GQ
            if g < NG - 1:
                odd = dram[t0:t0 + 2 * NODD * CHUNK, :].rearrange("(i a c) d -> i a c d", a=2, c=CHUNK)[:, 1]
                even = dram[t0 - PAST:t0 + GQ, :] if g else None
                if g:
                    even = even.rearrange("(i a c) d -> i a c d", a=2, c=CHUNK)[:, 1]
                    return [(odd, 0, NODD * CHUNK), (even, NODD * CHUNK, NEVEN * CHUNK)]
            pairs = (min(GQ, T - t0)) // (2 * CHUNK)
            both = dram[t0:t0 + pairs * 2 * CHUNK, :].rearrange("(i a c) d -> i a c d", a=2, c=CHUNK)
            tail = dram[t0 + pairs * 2 * CHUNK:min(t0 + GQ, T), :]
            return [(both[:, 1], 0, pairs * CHUNK), (both[:, 0], NODD * CHUNK, pairs * CHUNK),
                    (tail, (NODD + pairs) * CHUNK, tail.shape[0])]

        def stores(g, b):
            return sum(len(query_rows(out, i)) for i in range(g + 1) if i % 2 == b)

        def piece(n):
            return E - 1 - n // NPC, slice(n % NPC * PC, (n % NPC + 1) * PC)

        def split_slot(e):
            return e if e < NRING else e % 2

        def split_stores(n):
            return sum(piece(m)[0] >= NRING for m in range(n % PCS, n, PCS))

        NSPL = E * NPC

        XN_PER = 6
        S_SPL = 8

        def xn_tiles(s):
            return range(XCH + XN_PER * s, min(XCH + XN_PER * (s + 1), TT)) if s >= 0 else range(XCH)

        def base_tiles(g):
            return xn_tiles(g + 2) if g >= 0 else range(XCH + 2 * XN_PER)

        def pieces(s):
            return range(s - S_SPL, s - S_SPL + 1) if 0 <= s - S_SPL < NSPL else range(0)

        def x_bank(b):
            return {0: 2, 1: 4}.get(b, 7)

        def stage(eng, blocks, b, work):
            if 0 <= b < NB_MIN:
                work(b)
            elif NB_MIN <= b < NB:
                with eng.If(blocks > b):
                    work(b)

        block = ctx.enter_context(nc.Block())

        @block.sync
        def _(sp):
            for i in range(HC):
                sp.dma_start(q_scale[DH * i:DH * (i + 1), 1:2], dim_scale).then_inc(s_dim, 16)

            def rows(dram, i):
                first, last = PARTS[i]
                return dram[first * P:last * P, :].rearrange("(t p) d -> p t d", p=P)

            for i, (first, last) in enumerate(PARTS):
                sp.dma_start(x_all[:, first:last, :], rows(x, i)).then_inc(s_x[i], 16)
                if i == 0:
                    sp.dma_start(const[:, :], const_d).then_inc(s_const, 16)
            sp.dma_start(nwb[:, :], norm_w.to_broadcast([P, D])).then_inc(s_small, 16)
            sp.dma_start(al[:, 0:1], alpha.to_broadcast([P, 1])).then_inc(s_small, 16)
            sp.dma_start(rt_w[:, :, :], router_t.rearrange("(k p) e -> p k e", p=P)).then_inc(s_small, 16)
            sp.dma_start(pos_s[:, :, :], pos_t.rearrange("(k p) e -> p k e", p=P)).then_inc(s_small, 16)
            sp.dma_start(wrel_s, wrel.rearrange("(k p) e -> p k e", p=P)).then_inc(s_small, 16)
            for i, w in enumerate((wv, wpost)):
                sp.dma_start(vp_raw[:, i, :, :], w.rearrange("(k p) e -> p k e", p=P)).then_inc(s_vpw, 16)
            for i, w in enumerate((wq, wk)):
                sp.dma_start(att_w[:, i, :, :], w.rearrange("(k p) e -> p k e", p=P)).then_inc(s_attw, 16)

            def store_xn(i):
                first, last = PARTS[i]
                sp.wait_ge(s_xn, last)
                sp.dma_start(rows(xn_d, i), xn_all[:, first:last, :]).then_inc(s_xnst[i], 16)

            def store_base(i):
                first, last = PARTS[i]
                sp.wait_ge(s_bs, last)
                sp.dma_start(rows(base_d, i), base_all[:, first:last, :]).then_inc(s_bsst[i], 16)

            def rows_stored(done, g):
                for i, (first, last) in enumerate(PARTS):
                    if max(g * GQ - PAST, 0) < last * P and (g + 1) * GQ > first * P:
                        sp.wait_ge(done[i], 16)

            def store_normed(i):
                sp.wait_ge(s_nrm, (i + 1) * NRT)
                sp.dma_start(nrm_d[i * NRT * P:(i + 1) * NRT * P, :].rearrange("(t p) d -> p t d", p=P),
                             x_all[:, i * NRT:(i + 1) * NRT, :]).then_inc(s_nrmst, 16)

            def load_window(g):
                b = window(g)
                if g >= NWIN and b < NWIN:
                    sp.wait_ge(s_t, g - NWIN + 1)
                rows_stored(s_xnst, g)
                t0 = g * GQ - PAST
                if 0 < g < NG - 1:
                    src = xn_d[t0:t0 + GK, :].rearrange("(i a c) d -> a i c d", a=2, c=CHUNK)
                    for a in range(2):
                        sp.dma_start(win[a * HK:(a + 1) * HK, b, :], src[a]).then_inc(s_win[b], 16)
                    return
                for src, row, n in query_rows(xn_d, g):
                    sp.dma_start(win[PAST + row:PAST + row + n, b, :], src).then_inc(s_win[b], 16)
                if g:
                    sp.dma_start(win[0:PAST, b, :], xn_d[t0:t0 + PAST, :]).then_inc(s_win[b], 16)

            def load_base(g):
                if g >= 3:
                    sp.wait_ge(s_r2, g - 2)
                rows_stored(s_bsst, g)
                for src, row, n in query_rows(base_d, g):
                    sp.dma_start(base[row:row + n, g % 3, :], src).then_inc(s_xr[g % 3], 16)

            def flat_out(g):
                sp.wait_ge(s_bde, g + 1)
                sp.dma_start(bd_d[g], bd[0:GQ, g % 2, :, :].rearrange("q n h -> q (n h)")).then_inc(s_bdw[g % 2], 16)

            def shift_in(g):
                b = g % 2
                sp.wait_ge(s_bdw[b], 16 * (g // 2 + 1))
                if g >= 2:
                    sp.wait_ge(s_rep, g - 1)
                src = bd_d[g].rearrange("(n c) f -> n (c f)", c=CHUNK)[:, 0:CHUNK * CTX * H].rearrange(
                    "n (c f) -> n c f", c=CHUNK)
                r, half = NODD * CHUNK, PAST * H
                dst = shifted[:, b, :, :, :].rearrange("q a n h -> q (a n h)")
                sp.dma_start(dst[0:r, 0:half], src[0:NODD, :, half:2 * half]).then_inc(s_band[b], 16)
                sp.dma_start(dst[0:r, half:2 * half], src[0:NODD, :, 0:half]).then_inc(s_band[b], 16)
                sp.dma_start(dst[r:GQ, :], src[NODD:GB]).then_inc(s_band[b], 16)

            def load_raw(n):
                if n < NSPL:
                    e, cols = piece(n)
                    if n == 0:
                        sp.wait_ge(s_vpl, 1)
                    if n >= NST:
                        sp.wait_ge(s_spl, n - NST + 1)
                    sp.dma_start(raw[:, n % NST, :], w_raw[e, :, cols]).then_inc(s_raw[n % NST], 16)

            def load_expert(e, i):
                sp.wait_ge(s_w, 1 + 16 * ((e - NRING) * LPE + i))
                half, cols = i // NPC, slice(i % NPC * PC, (i % NPC + 1) * PC)
                sp.dma_start(w_ring[:, e % NRING, half, cols].bitcast(F32), w_split[e, :, half, cols]).then_inc(s_w, 16)

            store_xn(0)
            sp.wait_ge(s_ini, 4)
            for g in range(NWIN):
                load_window(g)
            store_xn(1)
            store_base(0)
            load_base(0)
            store_base(1)
            for s in range(NG + 4):
                if 0 <= s - (S_SPL - 3) < NST:
                    load_raw(s - (S_SPL - 3))
                for n in pieces(s - 2):
                    load_raw(n + NST)
                if s < NG:
                    flat_out(s)
                if NWIN <= s + 2 < NG:
                    load_window(s + 2)
                if 4 <= s:
                    g = s - 4
                    sp.wait_ge(s_r2, g + 1)
                    for dst, row, n in query_rows(out, g):
                        sp.dma_start(dst, res[row:row + n, g % 2, :]).then_inc(s_out[g % 2], 16)
                if 1 <= s - 1 < NG:
                    load_base(s - 1)
                if s < NG:
                    shift_in(s)
                for i in range(2, len(PARTS)):
                    if s == i:
                        store_xn(i)
                    if s == i + 2:
                        store_base(i)
                if 0 <= s - S_A < TT // NRT:
                    store_normed(s - S_A)
            sp.wait_ge(s_tab, 7)
            for i in range(PCS):
                sp.wait_ge(s_wst[i], 16 * split_stores(NSPL + i))
            for e in range(NRING, E):
                done = sp.value_load(first_blk[0:1, e - 2:e - 1], min_val=1, max_val=NB)
                sp.wait_ge(s_dn, done)
                for i in range(LPE):
                    load_expert(e, i)
            sp.wait_ge(s_w, 1 + 16 * (E - NRING) * LPE)
            for i in range(2):
                sp.wait_ge(s_out[i], 16 * stores(NG - 1, i))

        @block.gpsimd
        def _(pool):
            def add_base(t):
                pool.wait_ge(s_xn, t + 1)
                pool.tensor_tensor(base_all[:, t, :], x_all[:, t, :], xn_all[:, t, :], ALU.add).then_inc(s_bs, 1)

            def split(n):
                e, cols = piece(n)
                hi, lo = w_ring[:, split_slot(e), HI, cols], w_ring[:, split_slot(e), LO, cols]
                pool.wait_ge(s_hi, n + 1)
                pool.tensor_tensor(lo, raw[:, n % NST, :], hi.bitcast(F32), ALU.subtract).then_inc(s_spl, 1)
                if e >= NRING:
                    pool.wait_ge(s_spl, n + 1)
                    pool.dma_start(w_split[e, :, :, cols], w_ring[:, split_slot(e), :, cols].bitcast(F32)).then_inc(
                        s_wst[n % PCS], 16)

            def gather(b):
                if b >= NXG:
                    pool.wait_ge(s_xt, b - NXG + 1)
                pool.indirect_dma_start(
                    out=xg[:, b % NXG, :], out_offset=None, in_=nrm_d,
                    in_offset=bass.IndirectOffsetOnAxis(ap=gat_i[:, b:b + 1], axis=0),
                    bounds_check=T - 1, oob_is_err=False).then_inc(s_g[b % NXG], 16)

            pool.wait_ge(s_vph, 1)
            pool.tensor_tensor(vp_w[:, LO, :, :, :], vp_raw[:, :, :, :], vp_w[:, HI, :, :, :].bitcast(F32),
                               ALU.subtract).then_inc(s_vpl, 1)
            for t in base_tiles(-1):
                add_base(t)
            for g in range(NG):
                if g == NG - 4:
                    pool.wait_ge(s_tab, 7)
                    pool.wait_ge(s_nrmst, 16 * (TT // NRT))
                    pool.wait_ge(s_rel, 1)
                if g >= NG - 4:
                    gather(g - (NG - 4))
                if g == NG - 1:
                    for n in pieces(g + 2):
                        split(n)
                pool.wait_ge(s_ex, g + 1)
                pool.tensor_tensor(ex[0:GK, g % 2, 0:HM, :], ex[0:GK, g % 2, 0:HM, :],
                                   mask.rearrange("p (a n) -> p a n", a=1).to_broadcast([GK, HM, GQ]),
                                   ALU.mult).then_inc(s_mk, 1)
                for t in base_tiles(g):
                    add_base(t)
                for n in pieces(g + 2) if g < NG - 1 else ():
                    split(n)

            def scatter(b):
                pool.wait_ge(s_y, b + 1)
                pool.wait_ge(s_sc, 16 * b)
                pool.indirect_dma_start(
                    out=out, out_offset=bass.IndirectOffsetOnAxis(ap=sca_i[:, b:b + 1], axis=0),
                    in_=y[:, b % 2, :], in_offset=None, bounds_check=T - 1, oob_is_err=False,
                    compute_op=ALU.add).then_inc(s_sc, 16)

            for b in range(4, NXG):
                gather(b)
            blocks = pool.value_load(in_use[0:1, 0:1], min_val=NB_MIN, max_val=NB)
            for i in range(2):
                pool.wait_ge(s_out[i], 16 * stores(NG - 1, i))
            for b in range(NB):
                stage(pool, blocks, b + NXG, gather)
                stage(pool, blocks, b, scatter)
            total = pool.value_load(in_use[0:1, 1:2], min_val=16 * NB_MIN, max_val=16 * NB)
            pool.wait_ge(s_sc, total)

        @block.scalar
        def _(act):
            act.wait_ge(s_qs, 1)
            act.activation(q_scale[:, 3:4], q_scale[:, 2:3], ACT.Exp, scale=-1.0).then_inc(s_ea, 1)
            act.wait_ge(s_qs, 2)
            act.activation(q_scale[:, 5:6], q_scale[:, 4:5], ACT.Ln).then_inc(s_ea, 1)
            for i, c in enumerate((slice(0, X0), slice(X0, TT))):
                act.wait_ge(s_st, i + 1)
                act.activation(small[:, 0, c], small[:, 1, c], ACT.Sqrt).then_inc(s_sq, 1)
            act.wait_ge(s_vpw, 32)
            act.activation(vp_w[:, HI, :, :, :], vp_raw[:, :, :, :], ACT.Copy).then_inc(s_vph, 1)
            act.wait_ge(s_st, 3)
            act.activation(small[:, 3, :], small[:, 4, :], ACT.Sqrt).then_inc(s_sq, 1)

            def normed_evac(t):
                if t < TT:
                    act.wait_ge(s_nt, t + 1)
                    if t >= 2:
                        act.wait_ge(s_lg, t - 1)
                    act.activation(nrmT[:, t % 2, :, :], psum[:, 3, D:2 * D].rearrange("p (k n) -> p k n", k=KD),
                                   ACT.Copy).then_inc(s_nte, 1)

            def round_x(b):
                act.wait_ge(s_xt, b + 1)
                if b >= 2:
                    act.wait_ge(s_up, b - 1)
                loaded = act.value_load(blk_load[0:1, b:b + 1], min_val=1, max_val=1 + 16 * LPE * (E - NRING))
                act.wait_ge(s_w, loaded)
                act.activation(xT[:, b % 2, HI, :, :], psum[:, x_bank(b), 0:D].rearrange("p (k n) -> p k n", k=KD),
                               ACT.Copy).then_inc(s_xte, 1)

            act.wait_ge(s_qs, 3)
            for s in range(-1, NG + 4):
                tile = TPS * (s - 1) if 1 <= s < S_A else TT
                if s == S_A + 1:
                    act.wait_ge(s_ra, 1)
                    act.activation(tile8(2), tile8(1), ACT.Exp).then_inc(s_ea, 1)
                if 0 <= s < NG:
                    act.wait_ge(s_q, s + 1)
                    q_ps = psum[:, 2, D:D + KD * GQ].rearrange("p (k n) -> p k n", k=KD)
                    if s:
                        act.wait_ge(s_bd, s)
                    act.activation(qT[:, :, :], q_ps, ACT.Copy, scale=q_scale[:, 0:1])
                    if s == 0:
                        act.wait_ge(s_ini, 4)
                    if s >= 3:
                        act.wait_ge(s_s, s - 2)
                    for i in range(HC):
                        r = slice(DH * i, DH * (i + 1))
                        ins = act.activation(q_diag[r, s % 3, :, i, :], q_ps[r], ACT.Copy, scale=q_scale[r, 0:1])
                    ins.then_inc(s_qe, 1)
                    act.wait_ge(s_v, s + 1)
                    if s >= 4:
                        act.wait_ge(s_pv, s - 3)
                    act.activation(v1[0:GK, s % 4, :, 0:DH], psum[0:GK, 5, 0:D].rearrange("p (h n) -> p h n", h=H),
                                   ACT.Copy).then_inc(s_ve, 1)
                normed_evac(tile)
                if 0 <= s + 1 < NG:
                    act.wait_ge(s_t, s + 2)
                    if s >= 0:
                        act.wait_ge(s_v, s + 1)
                    turned = psum[:, 7, D:D + KD * GK].rearrange("p (k n) -> p k n", k=KD)
                    act.activation(xv[:, HI, :, :], turned, ACT.Copy)
                    act.activation(xnT[:, (s + 1) % 2, :, :], turned, ACT.Copy).then_inc(s_te, 1)
                normed_evac(tile + 1)
                if 0 <= s - 2 < NG:
                    g = s - 2
                    act.wait_ge(s_s, g + 1)
                    sc = psum[0:GK, 0:2, 0:HC * GQ]
                    act.activation(sc, sc, ACT.Tanh, scale=1.0 / SOFTCAP).then_inc(s_th, 1)
                    act.wait_ge(s_th, g + 1)
                    if g >= 2:
                        act.wait_ge(s_pv, g - 1)
                    act.activation(ex[0:GK, g % 2, :, :].rearrange("p (a h) n -> p a (h n)", a=2), sc, ACT.Exp,
                                   scale=SOFTCAP).then_inc(s_ex, 1)
                normed_evac(tile + 2)
                if s == NG:
                    round_x(0)

            def silu(b):
                act.wait_ge(s_gt, b + 1)
                if b >= 2:
                    act.wait_ge(s_h, b - 1)
                act.activation(sg[:, b % 2, :].rearrange("p (a n) -> p a n", a=2), psum[:, 0:2, 0:HALF],
                               ACT.Silu).then_inc(s_sg, 1)

            def round_h(b):
                act.wait_ge(s_ht, b + 1)
                if b >= 2:
                    act.wait_ge(s_dn, b - 1)
                act.activation(hT[:, b % 2, HI, :, :].rearrange("p (a k) n -> p a (k n)", a=2),
                               psum[:, 4:6, 0:3 * P], ACT.Copy).then_inc(s_hta, 1)

            blocks = act.value_load(in_use[0:1, 0:1], min_val=NB_MIN, max_val=NB)
            for b in range(NB + 1):
                stage(act, blocks, b, silu)
                stage(act, blocks, b + 1, round_x)
                stage(act, blocks, b - 1, round_h)

        @block.vector
        def _(dve):
            chain = [0]

            def link(ins):
                chain[0] += 1
                ins.then_inc(s_rt, 1)
                dve.wait_ge(s_rt, chain[0])

            def row(i, shape):
                return small[:, i, :].rearrange("p (t a) -> p t a", a=1).to_broadcast(shape)

            S8 = [P, TT, E]
            dve.memset(v1[:, :, :, DH:HV], 1.0).then_inc(s_ini, 1)
            dve.memset(q_diag[:, :, :, :, :].rearrange("p b k h n -> p (b k h n)"), 0.0).then_inc(s_ini, 1)
            dve.memset(win[:, 0, :], 0.0).then_inc(s_ini, 1)
            dve.memset(win[:, NWIN, :], 0.0).then_inc(s_ini, 1)
            link(dve.memset(rel_bd[:, :, :, :], 0.0))
            dve.wait_ge(s_dim, 16 * HC)
            link(dve.tensor_scalar(q_scale[:, 6:7], q_scale[:, 1:2], -1.0, None, ALU.mult))
            dve.tensor_tensor(q_scale[:, 2:3], q_scale[:, 1:2], q_scale[:, 6:7], ALU.max).then_inc(s_qs, 1)
            dve.wait_ge(s_ea, 1)
            dve.tensor_scalar(q_scale[:, 4:5], q_scale[:, 3:4], 1.0, None, ALU.add).then_inc(s_qs, 1)
            dve.wait_ge(s_ea, 2)
            dve.wait_ge(s_qs, 2)
            link(dve.tensor_scalar(q_scale[:, 6:7], q_scale[:, 4:5], -1.0, None, ALU.add))
            link(dve.tensor_scalar(q_scale[:, 7:8], q_scale[:, 6:7], 0.0, None, ALU.is_equal))
            link(dve.tensor_tensor(q_scale[:, 6:7], q_scale[:, 6:7], q_scale[:, 7:8], ALU.add))
            link(dve.reciprocal(q_scale[:, 6:7], q_scale[:, 6:7]))
            link(dve.scalar_tensor_tensor(out=q_scale[:, 6:7], in0=q_scale[:, 5:6], scalar=q_scale[:, 6:7],
                                          in1=q_scale[:, 7:8], op0=ALU.mult, op1=ALU.add))
            link(dve.tensor_tensor(q_scale[:, 6:7], q_scale[:, 6:7], q_scale[:, 3:4], ALU.mult))
            link(dve.scalar_tensor_tensor(out=q_scale[:, 6:7], in0=q_scale[:, 1:2], scalar=0.0,
                                          in1=q_scale[:, 6:7], op0=ALU.max, op1=ALU.add))
            dve.tensor_scalar(q_scale[:, 0:1], q_scale[:, 6:7], float(Q_SCALE), None, ALU.mult).then_inc(s_qs, 1)

            mean, var = mv[:, :, 0], mv[:, :, 1]

            def statistics(i, first, last):
                for t in range(first, last):
                    for n, part in enumerate(PARTS):
                        if t == part[0]:
                            dve.wait_ge(s_x[n], 16)
                    ins = dve.bn_stats(st6[:, t, :], x_all[:, t, :])
                link(ins)
                for t in range(first, last):
                    ins = dve.bn_aggr(mv[:, t, :], st6[:, t, :])
                link(ins)
                dve.tensor_scalar(small[:, 1, first:last], var[:, first:last], LN_EPS, None, ALU.add).then_inc(s_st, 1)
                dve.wait_ge(s_sq, i)
                link(dve.reciprocal(small[:, 2, first:last], small[:, 0, first:last]))

            def layernorm(t):
                dve.tensor_scalar(xn_all[:, t, :], x_all[:, t, :], mean[:, t:t + 1], small[:, 2, t:t + 1],
                                  ALU.subtract, ALU.mult).then_inc(s_xn, 1)

            statistics(1, 0, X0)
            for t in range(X0):
                layernorm(t)
            statistics(2, X0, TT)
            for t in range(X0, XCH):
                layernorm(t)
            link(dve.tensor_tensor(small[:, 5, :], small[:, 2, :], small[:, 2, :], ALU.mult))
            link(dve.tensor_tensor(small[:, 5, :], small[:, 5, :], var, ALU.mult))
            dve.tensor_scalar(small[:, 4, :], small[:, 5, :], RMS_EPS, None, ALU.add).then_inc(s_st, 1)
            dve.wait_ge(s_sq, 3)
            link(dve.reciprocal(small[:, 6, :], small[:, 3, :]))
            link(dve.tensor_tensor(small[:, 6, :], small[:, 6, :], small[:, 2, :], ALU.mult))

            dve.wait_ge(s_small, 16 * 5)

            def normed(t):
                dve.wait_ge(s_bs, t + 1)
                dve.tensor_scalar(x_all[:, t, :], x_all[:, t, :], mean[:, t:t + 1], small[:, 6, t:t + 1],
                                  ALU.subtract, ALU.mult).then_inc(s_n1, 1)
                dve.wait_ge(s_n1, t + 1)
                dve.tensor_tensor(x_all[:, t, :], x_all[:, t, :], nwb, ALU.mult).then_inc(s_nrm, 1)

            def round_piece(n):
                e, cols = piece(n)
                if n == 0:
                    for i in range(len(PARTS)):
                        dve.wait_ge(s_xnst[i], 16)
                        dve.wait_ge(s_bsst[i], 16)
                if n >= PCS:
                    dve.wait_ge(s_wst[n % PCS], 16 * split_stores(n))
                dve.wait_ge(s_raw[n % NST], 16 * (n // NST + 1))
                dve.tensor_copy(w_ring[:, split_slot(e), HI, cols], raw[:, n % NST, :]).then_inc(s_hi, 1)

            for k in range(KD):
                dve.wait_ge(s_rel, 1)
                for i in range(HC):
                    dve.tensor_copy(rel_bd[DH * i:DH * (i + 1), k, i, :],
                                    psum[DH * i:DH * (i + 1), 6, k * NPOS:(k + 1) * NPOS]).then_inc(s_qs, 1)

            def routing():
                dve.wait_ge(s_lg, TT)
                link(dve.tensor_copy(tile8(0), psum[:, 3, 0:TT * E].rearrange("p (t e) -> p t e", e=E)))
                link(dve.tensor_reduce(small[:, 0, :], tile8(0), AX_X, ALU.max))
                dve.tensor_tensor(tile8(1), tile8(0), row(0, S8), ALU.subtract).then_inc(s_ra, 1)
                yield
                dve.wait_ge(s_ea, 3)
                link(dve.tensor_reduce(small[:, 1, :], tile8(2), AX_X, ALU.add))
                link(dve.reciprocal(small[:, 1, :], small[:, 1, :]))
                link(dve.tensor_tensor(tile8(3), tile8(2), row(1, S8), ALU.mult))
                eidx = const[:, C_EXP:C_EXP + E].rearrange("p (a e) -> p a e", a=1).to_broadcast(S8)

                def choose(prob, best, hot):
                    link(dve.tensor_reduce(small[:, best, :], prob, AX_X, ALU.max))
                    link(dve.tensor_tensor(tile8(8), prob, row(best, S8), ALU.is_equal))
                    link(dve.scalar_tensor_tensor(out=tile8(9), in0=tile8(8), scalar=-float(E), in1=eidx,
                                                  op0=ALU.mult, op1=ALU.add))
                    link(dve.tensor_reduce(small[:, 7, :], tile8(9), AX_X, ALU.min))
                    link(dve.tensor_scalar(small[:, 7, :], small[:, 7, :], float(E), None, ALU.add))
                    link(dve.tensor_tensor(hot, eidx, row(7, S8), ALU.is_equal))

                choose(tile8(3), 0, tile8(10))
                yield
                link(dve.scalar_tensor_tensor(out=tile8(4), in0=tile8(10), scalar=-4.0, in1=tile8(3),
                                              op0=ALU.mult, op1=ALU.add))
                choose(tile8(4), 1, tile8(11))
                dve.tensor_tensor(tile8(12), tile8(10), tile8(11), ALU.add).then_inc(s_cnt, 1)
                yield
                link(dve.tensor_scalar(al[:, 1:2], al[:, 0:1], ALPHA_LO, ALPHA_HI, ALU.max, ALU.min))
                link(dve.tensor_tensor(small[:, 2, :], small[:, 0, :], small[:, 1, :], ALU.add))
                link(dve.reciprocal(small[:, 2, :], small[:, 2, :]))
                link(dve.tensor_scalar(small[:, 2, :], small[:, 2, :], al[:, 1:2], None, ALU.mult))
                link(dve.tensor_tensor(small[:, 0, :], small[:, 0, :], small[:, 2, :], ALU.mult))
                link(dve.tensor_tensor(small[:, 1, :], small[:, 1, :], small[:, 2, :], ALU.mult))
                dve.wait_ge(s_cnt, 3)
                link(dve.tensor_copy(tile8(13), psum[:, 3, TT * E:2 * TT * E].rearrange("p (t e) -> p t e", e=E)))
                for e in range(E):
                    ins = dve.tensor_tensor_scan(tile8(14)[:, :, e], ones[:, 0:TT], tile8(13)[:, :, e], 0.0,
                                                 ALU.mult, ALU.add)
                link(ins)
                yield
                link(dve.tensor_scalar(e8i[:, 0, :], tile8(14)[:, TT - 1, :], float(P - 1), float(P), ALU.add, ALU.max))
                link(dve.tensor_scalar(e8i[:, 1, :], e8i[:, 0, :], 7, 7, ALU.logical_shift_right, ALU.logical_shift_left))
                link(dve.tensor_copy(e8[:, 0, :], e8i[:, 1, :]))
                link(dve.tensor_tensor_scan(e8[:, 1, :], ones[:, 0:E], e8[:, 0, :], 0.0, ALU.mult, ALU.add))
                link(dve.tensor_tensor(e8[:, 2, :], e8[:, 1, :], e8[:, 0, :], ALU.subtract))
                link(dve.tensor_copy(e8i[:, 1, :], e8[:, 1, :]))
                dve.tensor_scalar(in_use[:, 0:1], e8i[0:1, 1, E - 1:E], 7, None, ALU.logical_shift_right).then_inc(s_tab, 1)
                dve.tensor_scalar(in_use[:, 1:2], e8i[0:1, 1, E - 1:E], 3, None, ALU.logical_shift_right).then_inc(s_tab, 1)
                link(dve.tensor_copy(e8i[:, 2, :], e8[:, 2, :]))
                dve.tensor_scalar(first_blk[:, :], e8i[0:1, 2, :], 7, None, ALU.logical_shift_right).then_inc(s_tab, 1)
                link(dve.tensor_tensor(tile8(14), tile8(14), tile8(13), ALU.subtract))
                link(dve.tensor_tensor(tile8(14), tile8(14),
                                       e8[:, 2, :].rearrange("p (a e) -> p a e", a=1).to_broadcast(S8), ALU.add))
                link(dve.tensor_tensor(tile8(14), psum[:, 3, 0:TT * E].rearrange("p (t e) -> p t e", e=E), tile8(14),
                                       ALU.add))
                for k in range(2):
                    yield
                    link(dve.tensor_tensor(tile8(8), tile8(14), tile8(10 + k), ALU.mult))
                    link(dve.tensor_reduce(small[:, 3, :], tile8(8), AX_X, ALU.add))
                    link(dve.tensor_copy(sl_i[:, 0, :], small[:, 3, :]))
                    link(dve.tensor_scalar(sl_i[:, 1, :], sl_i[:, 0, :], P - 1, None, ALU.bitwise_and))
                    link(dve.tensor_scalar(sl_i[:, 2, :], sl_i[:, 0, :], 7, 7, ALU.logical_shift_right,
                                           ALU.logical_shift_left))
                    link(dve.tensor_copy(small[:, 4 + k, :], sl_i[:, 1, :]))
                    link(dve.tensor_copy(small[:, 6 + k, :], sl_i[:, 2, :]))
                link(dve.tensor_tensor(be[:, :, :],
                                       const[0:1, C_BLK:C_BLK + NB].rearrange("p (n a) -> p n a", a=1).to_broadcast(
                                           [1, NB, E]),
                                       e8[0:1, 1, :].rearrange("p (a e) -> p a e", a=1).to_broadcast([1, NB, E]),
                                       ALU.is_ge))
                link(dve.tensor_reduce(bef[:, 0, :], be[:, :, :], AX_X, ALU.add))
                link(dve.tensor_scalar(bef[:, 0, :], bef[:, 0, :], float(E - 1), None, ALU.min))
                link(dve.tensor_scalar(bef[:, 3, :], bef[:, 0, :], 1.0 - NRING, 0.0, ALU.add, ALU.max))
                dve.tensor_scalar(blk_load[:, :], bef[:, 3, :], 16.0 * LPE, 1.0, ALU.mult, ALU.add).then_inc(s_tab, 1)
                link(dve.tensor_scalar(bef[:, 1, :], bef[:, 0, :], float(NRING), -float(NRING), ALU.is_ge, ALU.mult))
                link(dve.tensor_scalar(bef[:, 2, :], bef[:, 0, :], 2.0 * NRING, -float(NRING), ALU.is_ge, ALU.mult))
                link(dve.tensor_tensor(bef[:, 0, :], bef[:, 0, :], bef[:, 1, :], ALU.add))
                dve.tensor_tensor(blk_slot[:, :], bef[:, 0, :], bef[:, 2, :], ALU.add).then_inc(s_w, 1)
                blk = const[:, C_BLK:C_BLK + NB]
                for n in range(2 * TT):
                    if n % OPS in (0, 3):
                        yield
                    k, t = n // TT, n % TT
                    if n >= NOH:
                        dve.wait_ge(s_inv, n - NOH + 1)
                    dve.tensor_scalar(oh[:, n % NOH, :], iota, small[:, 4 + k, t:t + 1], None, ALU.is_equal)
                    dve.tensor_scalar(ohb[:, n % NOH, 0, :], blk, small[:, 6 + k, t:t + 1],
                                      const[:, C_TOK + t:C_TOK + t + 1], ALU.is_equal, ALU.mult)
                    dve.tensor_scalar(ohb[:, n % NOH, 1, :], blk, small[:, 6 + k, t:t + 1], small[:, k, t:t + 1],
                                      ALU.is_equal, ALU.mult).then_inc(s_oh, 1)
                yield
                dve.wait_ge(s_inv, 2 * TT)
                link(dve.tensor_copy(tab[:, 0, :], psum[:, 3, 0:NB]))
                dve.tensor_copy(slot_w[:, :], psum[:, 3, NB:2 * NB]).then_inc(s_tab, 1)
                link(dve.tensor_scalar(tab[:, 1, :], tab[:, 0, :], -1.0, 0.0, ALU.add, ALU.max))
                dve.tensor_copy(gat_i[:, :], tab[:, 1, :]).then_inc(s_tab, 1)
                link(dve.tensor_scalar(tab[:, 2, :], tab[:, 0, :], 0.0, const[:, C_OOB:C_OOB + 1], ALU.is_equal,
                                       ALU.mult))
                link(dve.tensor_tensor(tab[:, 2, :], tab[:, 2, :], tab[:, 0, :], ALU.add))
                dve.tensor_scalar(sca_i[:, :], tab[:, 2, :], -1.0, None, ALU.add).then_inc(s_tab, 1)
                yield

            def hidden(b):
                dve.wait_ge(s_up, b + 1)
                dve.wait_ge(s_sg, b + 1)
                if b >= 2:
                    dve.wait_ge(s_ht, b - 1)
                dve.tensor_tensor(hb[:, b % 2, 0:HID].rearrange("p (a n) -> p a n", a=2), psum[:, 2:4, 0:HALF],
                                  sg[:, b % 2, :].rearrange("p (a n) -> p a n", a=2), ALU.mult)
                dve.tensor_tensor(hb[:, b % 2, HID:HIDP], psum[:, 3, HALF - REST:HALF], sg[:, b % 2, HID - REST:HID],
                                  ALU.mult).then_inc(s_h, 1)

            def rest_x(b):
                dve.wait_ge(s_xte, b + 1)
                dve.tensor_tensor(xT[:, b % 2, LO, :, :], psum[:, x_bank(b), 0:D].rearrange("p (k n) -> p k n", k=KD),
                                  xT[:, b % 2, HI, :, :].bitcast(F32), ALU.subtract).then_inc(s_xtl, 1)

            route = routing()
            steps = [S_A, S_A + 1, S_A + 2, S_HOT, S_HOT + 1, S_HOT + 2, S_HOT + 3]
            steps += list(range(S_OH, S_TAB + 1))

            def rest_v(g):
                dve.wait_ge(s_te, g + 1)
                dve.tensor_tensor(xv[:, LO, :, :], psum[:, 7, D:D + KD * GK].rearrange("p (k n) -> p k n", k=KD),
                                  xv[:, HI, :, :].bitcast(F32), ALU.subtract).then_inc(s_xvl, 1)

            def repeat(g):
                dve.wait_ge(s_band[g % 2], 48 * (g // 2 + 1))
                if g:
                    dve.wait_ge(s_s, g)
                for a in range(2):
                    rel = shifted[0:GQ, g % 2, a, :, :].rearrange("p (r n) h -> p h r n", r=1)
                    ins = dve.tensor_copy(spread[0:GQ, :, a, :, :],
                                          rel.to_broadcast([GQ, H, HK // CHUNK, CHUNK]))
                ins.then_inc(s_rep, 1)

            rest_v(0)
            for s in range(NG + 4):
                if 0 <= s - 2 < NG - 1:
                    repeat(s - 2)
                for n in pieces(s):
                    round_piece(n)
                if s < NG:
                    dve.wait_ge(s_k, s + 1)
                    if s >= 3:
                        dve.wait_ge(s_s, s - 2)
                    dve.tensor_scalar(kT[:, s % 3, :, :], psum[:, 4, 0:KD * GK].rearrange("p (k n) -> p k n", k=KD),
                                      float(K_SCALE), None, ALU.mult).then_inc(s_ke, 1)
                if 0 <= s - 3 < NG:
                    g = s - 3
                    dve.wait_ge(s_ex, g + 1)
                    dve.tensor_tensor(ex[0:GK, g % 2, HM:H, :], ex[0:GK, g % 2, HM:H, :],
                                      mask.rearrange("p (a n) -> p a n", a=1).to_broadcast([GK, H - HM, GQ]),
                                      ALU.mult).then_inc(s_mkd, 1)
                if 0 <= s - 4 < NG:
                    g = s - 4
                    loads = sum(len(query_rows(base_d, i)) for i in range(g + 1) if i % 3 == g % 3)
                    dve.wait_ge(s_po, g + 1)
                    dve.wait_ge(s_xr[g % 3], 16 * loads)
                    if g >= 2:
                        dve.wait_ge(s_out[g % 2], 16 * stores(g - 2, g % 2))
                    dve.tensor_tensor(res[0:GQ, g % 2, :], psum[0:GQ, 7, 0:D], base[0:GQ, g % 3, :],
                                      ALU.add).then_inc(s_r2, 1)
                for t in range(TPS * s, min(TPS * (s + 1), TT)):
                    normed(t)
                for t in xn_tiles(s):
                    layernorm(t)
                if s in steps:
                    next(route)
                if s == NG:
                    repeat(NG - 1)
                if 0 <= s - 3 < NG:
                    g = s - 3
                    dve.wait_ge(s_pv, g + 1)
                    pv = psum[0:GQ, 6, 0:H * HV].rearrange("p (h n) -> p h n", h=H)
                    dve.reciprocal(rden[0:GQ, :], pv[:, :, DH:HV].rearrange("p h n -> p (h n)")).then_inc(s_rc, 1)
                    dve.wait_ge(s_rc, g + 1)
                    if g:
                        dve.wait_ge(s_ot, g)
                    dve.tensor_tensor(o_sb[0:GQ, :, :], pv[:, :, 0:DH],
                                      rden[0:GQ, :].rearrange("p (h n) -> p h n", n=1).to_broadcast([GQ, H, DH]),
                                      ALU.mult).then_inc(s_o, 1)
                if s < NG:
                    dve.wait_ge(s_bd, s + 1)
                    if s >= 2:
                        dve.wait_ge(s_bdw[s % 2], 16 * (s // 2))
                    dve.tensor_copy(bd[0:GQ, s % 2, :, :],
                                    psum[0:GQ, 4, D:D + H * NPOS].rearrange("p (h n) -> p n h", h=H)).then_inc(s_bde, 1)
                if S_OH <= s < S_TAB:
                    next(route)
                if s + 1 < NG:
                    rest_v(s + 1)
                if 0 <= s - 3 < NG:
                    g = s - 3
                    dve.wait_ge(s_ot, g + 1)
                    if g:
                        dve.wait_ge(s_po, g)
                    o_ps = psum[:, 6, 0:KD * GQ].rearrange("p (k n) -> p k n", k=KD)
                    dve.tensor_copy(oT_hi[:, :, :], o_ps).then_inc(s_oth, 1)
                    dve.wait_ge(s_oth, g + 1)
                    dve.tensor_tensor(oT_lo[:, :, :], o_ps, oT_hi[:, :, :].bitcast(F32), ALU.subtract).then_inc(s_ote, 1)
                if s == NG:
                    rest_x(0)
                if s == NG + 2:
                    hidden(0)
                    rest_x(1)

            def rest_h(b):
                dve.wait_ge(s_hta, b + 1)
                dve.tensor_tensor(hT[:, b % 2, LO, :, :].rearrange("p (a k) n -> p a (k n)", a=2), psum[:, 4:6, 0:3 * P],
                                  hT[:, b % 2, HI, :, :].bitcast(F32).rearrange("p (a k) n -> p a (k n)", a=2),
                                  ALU.subtract).then_inc(s_htl, 1)
                dve.wait_ge(s_htl, b + 1)
                dve.tensor_copy(hT[REST:P, b % 2, HI, HCH - 1, :],
                                hT[REST:P, b % 2, LO, HCH - 1, :].bitcast(F32)).then_inc(s_htb, 1)

            def weigh(b):
                dve.wait_ge(s_dn, b + 1)
                if b >= 2:
                    dve.wait_ge(s_sc, 16 * (b - 1))
                dve.tensor_scalar(y[:, b % 2, :], psum[:, 6, 0:D], slot_w[:, b:b + 1], None, ALU.mult).then_inc(s_y, 1)

            blocks = dve.value_load(in_use[0:1, 0:1], min_val=NB_MIN, max_val=NB)
            for b in range(1, NB + 2):
                stage(dve, blocks, b, hidden)
                stage(dve, blocks, b + 1, rest_x)
                stage(dve, blocks, b - 1, rest_h)
                stage(dve, blocks, b - 2, weigh)

        @block.tensor
        def _(pe):
            def mm(out_ap, lhs, rhs, first, last):
                return pe.matmul(out_ap, lhs, rhs, start=first, stop=last)

            pe.wait_ge(s_small, 16 * 5)
            pe.wait_ge(s_const, 16)
            for m in range(KD):
                for k in range(KD):
                    ins = mm(psum[:, 6, m * NPOS:(m + 1) * NPOS], wrel_s[:, k, m * P:(m + 1) * P], pos_s[:, k, :],
                             k == 0, k == KD - 1)
            ins.then_inc(s_rel, 1)

            def logits(t):
                if 1 <= t <= TT:
                    u = t - 1
                    pe.wait_ge(s_nte, u + 1)
                    for k in range(KD):
                        ins = mm(psum[:, 3, u * E:(u + 1) * E], nrmT[:, u % 2, k, :], rt_w[:, k, :], k == 0, k == KD - 1)
                    ins.then_inc(s_lg, 1)
                if t < TT:
                    pe.wait_ge(s_nrm, t + 1)
                    for k in range(KD):
                        ins = pe.transpose(psum[:, 3, D + k * P:D + (k + 1) * P], x_all[:, t, k * P:(k + 1) * P], ident)
                    ins.then_inc(s_nt, 1)

            def count():
                pe.wait_ge(s_cnt, 1)
                hot = spare[:, 12, :]
                mm(psum[:, 3, 0:TT * E], tri, hot, True, True).then_inc(s_cnt, 1)
                mm(psum[:, 3, TT * E:2 * TT * E], ones, hot, True, True).then_inc(s_cnt, 1)

            def tables(first, last):
                for n in range(first, min(last, 2 * TT)):
                    pe.wait_ge(s_oh, n + 1)
                    mm(psum[:, 3, 0:2 * NB], oh[:, n % NOH, :], ohb[:, n % NOH, :, :].rearrange("p a n -> p (a n)"),
                       n == 0, n == 2 * TT - 1).then_inc(s_inv, 1)

            def turn(g):
                b = window(g)
                loads = sum(len(query_rows(xn_d, i)) + (i > 0) if i in (0, NG - 1) else 2
                            for i in range(g + 1) if window(i) == b)
                pe.wait_ge(s_win[b], 16 * loads)
                if g:
                    pe.wait_ge(s_te, g)
                    pe.wait_ge(s_xvl, g)
                if g >= 5:
                    pe.wait_ge(s_r2, g - 4)
                for k in range(KD):
                    ins = pe.transpose(psum[:, 7, D + k * GK:D + (k + 1) * GK], win[0:GK, b, k * P:(k + 1) * P],
                                       ident[0:GK, 0:GK])
                ins.then_inc(s_t, 1)

            def turn_x(b):
                pe.wait_ge(s_g[b % NXG], 16 * (b // NXG + 1))
                if b:
                    pe.wait_ge(s_xtl, b)
                if b == 2:
                    pe.wait_ge(s_r2, NG)
                for k in range(KD):
                    ins = pe.transpose(psum[:, x_bank(b), k * P:(k + 1) * P], xg[:, b % NXG, k * P:(k + 1) * P], ident)
                ins.then_inc(s_xt, 1)

            slots = [None] * NB

            def gate_up(b):
                slots[b] = pe.value_load(blk_slot[0:1, b:b + 1], min_val=0, max_val=NRING - 1)
                pe.wait_ge(s_xtl, b + 1)
                for j in (0, 1, 2, 3) if b else (2, 3, 0, 1):
                    if b and j == 0:
                        pe.wait_ge(s_sg, b)
                    if b and j == 2:
                        pe.wait_ge(s_h, b)
                    if not b and j == 0:
                        pe.wait_ge(s_ex, NG)
                    for k in range(KD):
                        for px, pw in PASSES:
                            first = (k * 2 * HID) + j * HALF
                            w = w_ring[:, bass.ds(slots[b], 1), pw, first:first + HALF].rearrange("p s n -> p (s n)")
                            ins = mm(psum[:, j, 0:HALF], xT[:, b % 2, px, k, :], w,
                                     k == 0 and (px, pw) == PASSES[0], k == KD - 1 and (px, pw) == PASSES[-1])
                    if b and j == 1:
                        ins.then_inc(s_gt, 1)
                    if not b and j == 3:
                        ins.then_inc(s_up, 1)
                ins.then_inc(s_up if b else s_gt, 1)

            def turn_h(b):
                pe.wait_ge(s_h, b + 1)
                if b:
                    pe.wait_ge(s_hta, b)
                    pe.wait_ge(s_htb, b)
                for c in range(HCH):
                    ins = pe.transpose(psum[:, 4 + c // 3, (c % 3) * P:(c % 3 + 1) * P], hb[:, b % 2, c * P:(c + 1) * P],
                                       ident)
                ins.then_inc(s_ht, 1)

            def down(b):
                pe.wait_ge(s_hta, b + 1)
                pe.wait_ge(s_htb, b + 1)
                if b:
                    pe.wait_ge(s_y, b)
                slot = slots[b] if b < NB_MIN else pe.value_load(blk_slot[0:1, b:b + 1], min_val=0, max_val=NRING - 1)
                for c in range(HCH):
                    for ph, pw in PASSES if c < HCH - 1 else PASSES[:2]:
                        first = GU_COLS + c * D
                        w = w_ring[:, bass.ds(slot, 1), pw, first:first + D].rearrange("p s n -> p (s n)")
                        ins = mm(psum[:, 6, 0:D], hT[:, b % 2, ph, c, :], w,
                                 c == 0 and (ph, pw) == PASSES[0], c == HCH - 1 and (ph, pw) == PASSES[1])
                ins.then_inc(s_dn, 1)

            def values(g):
                pe.wait_ge(s_mkd, g + 1)
                pe.wait_ge(s_ve, g + 1)
                if g:
                    pe.wait_ge(s_ote, g)
                for h in (*range(HM, H), *range(HM)):
                    if h == 0:
                        pe.wait_ge(s_mk, g + 1)
                    ins = mm(psum[0:GQ, 6, h * HV:(h + 1) * HV], ex[0:GK, g % 2, h, :], v1[0:GK, g % 4, h, :],
                             True, True)
                ins.then_inc(s_pv, 1)

            def project(g):
                pe.wait_ge(s_ote, g + 1)
                pe.wait_ge(s_te, min(g + 5, NG))
                pe.wait_ge(s_xvl, min(g + 5, NG))
                if g:
                    pe.wait_ge(s_r2, g)
                for k in range(KD):
                    for po, pw in PASSES:
                        ins = mm(psum[0:GQ, 7, 0:D], (oT_hi, oT_lo)[po][:, k, :], vp_w[:, pw, WP, k, :],
                                 k == 0 and (po, pw) == PASSES[0], k == KD - 1 and (po, pw) == PASSES[-1])
                ins.then_inc(s_po, 1)

            def scores(g):
                pe.wait_ge(s_rep, g + 1)
                if g:
                    pe.wait_ge(s_ex, g)
                for k in range(KD):
                    for i in range(HC):
                        pe.matmul(psum[0:GK, k, i * GQ:(i + 1) * GQ],
                                  spread[0:GQ, HC * k + i, :, :, :].rearrange("p a r n -> p (a r n)"),
                                  ident[0:GQ, 0:GQ], start=i == 0, stop=False, is_transpose=True)
                    ins = mm(psum[0:GK, k, 0:HC * GQ], kT[:, g % 3, k, :],
                             q_diag[:, g % 3, k, :, :].rearrange("p h n -> p (h n)"), False, True)
                ins.then_inc(s_s, 1)

            def turn_out(g):
                pe.wait_ge(s_o, g + 1)
                for k in range(KD):
                    ins = pe.transpose(psum[:, 6, k * GQ:(k + 1) * GQ],
                                       o_sb[0:GQ, HC * k:HC * (k + 1), :].rearrange("p h n -> p (h n)"),
                                       ident[0:GQ, 0:GQ])
                ins.then_inc(s_ot, 1)

            pe.wait_ge(s_attw, 32)
            pe.wait_ge(s_vpl, 1)
            pe.wait_ge(s_qs, 3 + KD * HC)
            pe.wait_ge(s_ini, 4)
            turn(0)
            for s in range(NG + 4):
                tile = TPS * (s - 1) if 1 <= s <= S_A else TT + 1
                if s == S_HOT:
                    count()
                if s > S_OH:
                    tables(OPS * (s - S_OH - 1), OPS * (s - S_OH))
                if s < NG:
                    src = xnT[:, s % 2, :, :]
                    pe.wait_ge(s_te, s + 1)
                    if s:
                        pe.wait_ge(s_qe, s)
                    for m in range(KD):
                        for k in range(KD):
                            ins = mm(psum[:, 2, D + m * GQ:D + (m + 1) * GQ], att_w[:, WQ, k, m * P:(m + 1) * P],
                                     src[:, k, PAST:GK], k == 0, k == KD - 1)
                    ins.then_inc(s_q, 1)
                    if s:
                        pe.wait_ge(s_bde, s)
                    for m in range(KD):
                        for k in range(KD):
                            ins = mm(psum[:, 4, m * GK:(m + 1) * GK], att_w[:, WK, k, m * P:(m + 1) * P],
                                     src[:, k, :], k == 0, k == KD - 1)
                    ins.then_inc(s_k, 1)
                    if s:
                        pe.wait_ge(s_ve, s)
                    pe.wait_ge(s_xvl, s + 1)
                    for k in range(KD):
                        for px, pw in PASSES:
                            ins = mm(psum[0:GK, 5, 0:D], xv[:, px, k, :], vp_w[:, pw, WV, k, :],
                                     k == 0 and (px, pw) == PASSES[0], k == KD - 1 and (px, pw) == PASSES[-1])
                    ins.then_inc(s_v, 1)
                logits(tile)
                if s >= NG and s - 2 < NG:
                    scores(s - 2)
                if s == NG:
                    pe.wait_ge(s_tab, 7)
                    pe.wait_ge(s_nrmst, 16 * (TT // NRT))
                    pe.wait_ge(s_te, NG)
                    pe.wait_ge(s_qe, NG)
                    turn_x(0)
                if s == NG + 2:
                    pe.wait_ge(s_spl, NSPL - 1)
                    gate_up(0)
                    pe.wait_ge(s_bde, NG)
                    pe.wait_ge(s_ke, NG)
                    turn_x(1)
                if 0 <= s - 4 < NG:
                    project(s - 4)
                if 0 <= s - 3 < NG:
                    values(s - 3)
                if s + 1 < NG:
                    turn(s + 1)
                logits(tile + 1)
                if s < NG:
                    pe.wait_ge(s_qe, s + 1)
                    pe.wait_ge(s_ke, s + 1)
                    for k in range(KD):
                        ins = mm(psum[0:GQ, 4, 256 + k * HC * NPOS:256 + (k + 1) * HC * NPOS], qT[:, k, :],
                                 rel_bd[:, k, :, :].rearrange("p h n -> p (h n)"), True, True)
                    ins.then_inc(s_bd, 1)
                if 0 <= s - 2 and s < NG:
                    scores(s - 2)
                logits(tile + 2)
                if 0 <= s - 3 < NG:
                    turn_out(s - 3)

            pe.wait_ge(s_spl, NSPL)
            blocks = pe.value_load(in_use[0:1, 0:1], min_val=NB_MIN, max_val=NB)
            for b in range(1, NB + 2):
                stage(pe, blocks, b, gate_up)
                stage(pe, blocks, b - 1, turn_h)
                stage(pe, blocks, b + 1, turn_x)
                stage(pe, blocks, b - 2, down)


def weights(gate_up, down):
    w = np.zeros((E, P, WC), gate_up.dtype)
    w[:, :, :GU_COLS] = gate_up.reshape(E, 2 * HID, KD, P).transpose(0, 3, 2, 1).reshape(E, P, GU_COLS)
    dn = np.concatenate([down, down[:, :, HID - REST:]], axis=2)
    w[:, :, GU_COLS:] = dn.reshape(E, D, HCH, P).transpose(0, 3, 2, 1).reshape(E, P, HCH * D)
    return w


def kernel(**inputs):
    import concourse.bacc as _bacc
    from concourse.bass_utils import run_bass_kernel_spmd as _run

    def arr(name):
        return np.asarray(inputs[name])

    def turned(a, *axes):
        return np.ascontiguousarray(np.transpose(a, axes))

    arrays = {
        "x": np.ascontiguousarray(arr("L0_attn_hidden_states").reshape(T, D)),
        "pos_t": turned(arr("L0_attn_position_embeddings"), 1, 0),
        "wq": turned(arr("L0_attn_Wq"), 1, 0),
        "wk": turned(arr("L0_attn_Wk"), 1, 0),
        "wv": turned(arr("L0_attn_Wv"), 1, 0),
        "wpost": turned(arr("L0_attn_Wpost"), 1, 0),
        "wrel": turned(arr("L0_attn_Wrel"), 1, 0),
        "dim_scale": np.ascontiguousarray(arr("L0_attn_per_dim_scale").reshape(DH, 1)),
        "norm_w": np.ascontiguousarray(arr("L0_ffn_norm_weight").reshape(1, D)),
        "router_t": turned(arr("L0_ffn_router_weight"), 1, 0),
        "w_raw": weights(arr("L0_ffn_gate_up_weight"), arr("L0_ffn_down_weight")),
        "alpha": np.ascontiguousarray(arr("L0_ffn_residual_alpha").reshape(1, 1)),
        "const": constants(),
    }
    nc = _bacc.Bacc("TRN2", target_bir_lowering=False, num_devices=1)
    args = [nc.dram_tensor("in_" + n, a.shape, mybir.dt.from_np(a.dtype), kind="ExternalInput").ap() for n, a in arrays.items()]
    args.append(nc.dram_tensor("xn_d", (T, D), F32, kind="Internal").ap())
    args.append(nc.dram_tensor("base_d", (T, D), F32, kind="Internal").ap())
    args.append(nc.dram_tensor("nrm_d", (T, D), F32, kind="Internal").ap())
    args.append(nc.dram_tensor("bd_d", (NG, GQ, NPOS * H), F32, kind="Internal").ap())
    args.append(nc.dram_tensor("w_split", (E, P, 2, WC), F32, kind="Internal").ap())
    args.append(nc.dram_tensor("out", (T, D), F32, kind="ExternalOutput").ap())
    program(nc, *args)
    r = _run(nc, [{"in_" + n: a for n, a in arrays.items()}], core_ids=[0])
    return r.results[0]["out"].reshape(1, T, D)
```
